# Optimizing a Trainium2 kernel written in Bass

```python
import numpy as np
import jax
import jax.numpy as jnp

def _softmax(x, axis=-1):
    return jax.nn.softmax(x, axis=axis)

def _gelu(x):
    return jax.nn.gelu(x, approximate=True)

def _silu(x):
    return jax.nn.silu(x)

def _sigmoid(x):
    return jax.nn.sigmoid(x)

def _layernorm(x, axis=-1, eps=1e-05):
    m = jnp.mean(x, axis=axis, keepdims=True)
    v = jnp.var(x, axis=axis, keepdims=True)
    return (x - m) / jnp.sqrt(v + eps)

def _scatter_add(tgt, idx, src, axis=0):
    return tgt.at[idx].add(src)

def _segment_sum(src, seg, n):
    return jax.ops.segment_sum(src, seg, n)
kernel_name = 'mk_cond_resid_d2_seqx_r8_66e575'

def setup_inputs(seed: int=0):
    np.random.seed(seed)
    _w = jnp.asarray

    def _rec_inputs():
        import jax
        import jax.numpy as jnp
        _rk = jax.random.key(seed)
        x = -7.109e-05 + 0.9999 * jax.random.normal(jax.random.fold_in(_rk, 1), (8, 128, 512), jnp.float32)
        _lenS = 128 - jax.random.randint(jax.random.fold_in(_rk, 7), (8,), 0, max(1, 128 // 4) + 1, jnp.int32)
        _lenS2 = 128 - jax.random.randint(jax.random.fold_in(_rk, 8), (8,), 0, max(1, 128 // 4) + 1, jnp.int32)
        itok_B_0_15 = jax.random.randint(jax.random.fold_in(_rk, 11), (8,), 0, 16, jnp.int32)
        itok_Bx16_0_63 = jax.random.randint(jax.random.fold_in(_rk, 12), (8, 16), 0, 64, jnp.int32)
        itok_B_207_1644 = jax.random.randint(jax.random.fold_in(_rk, 13), (8,), 207, 1645, jnp.int32)
        return (x, itok_B_0_15, itok_Bx16_0_63, itok_B_207_1644)
    x, itok_B_0_15, itok_Bx16_0_63, itok_B_207_1644 = _rec_inputs()

    def _L0_cond_setup():
        import jax, jax.numpy as jnp
        import numpy as np
        MAX_LORAS = 16
        IN, OUT = (512, 512)
        B, S = (8, 256)
        key = jax.random.key(seed)
        k1, k2, k3 = jax.random.split(key, 3)
        x = jax.random.normal(k1, (B, S, IN), dtype=jnp.float32)
        adapter_ids = jax.random.randint(k2, (B,), 0, MAX_LORAS)
        weight = jax.random.normal(k3, (MAX_LORAS, OUT, IN), dtype=jnp.float32) * 0.02
        return {'x': x, 'adapter_ids': adapter_ids, 'weight': weight}
    _L0_cond_all = _L0_cond_setup()
    _L0_cond_in = {k: v for k, v in _L0_cond_all.items() if k in ('weight',)}
    del _L0_cond_all

    def _L1_cond_setup():
        import jax, jax.numpy as jnp
        import numpy as np
        B, S, HID = (4, 128, 512)
        D, HQ, HK = (128, 32, 8)
        PAGES, PSIZE, NPP = (64, 32, 16)
        THETA = 10000.0
        EPS = 1e-06
        SCALE = 1.0 / float(np.sqrt(D))

        def _rmsnorm(t, w):
            var = jnp.mean(t * t, axis=-1, keepdims=True)
            return t * jax.lax.rsqrt(var + EPS) * w

        def _rope(t, pos):
            inv_freq = 1.0 / THETA ** (jnp.arange(0, D, 2, dtype=jnp.float32) / D)
            freqs = pos[..., None].astype(jnp.float32) * inv_freq
            cos = jnp.cos(freqs)[:, :, None, :]
            sin = jnp.sin(freqs)[:, :, None, :]
            t1, t2 = (t[..., :D // 2], t[..., D // 2:])
            return jnp.concatenate([t1 * cos - t2 * sin, t2 * cos + t1 * sin], axis=-1)
        key = jax.random.key(seed)
        ks = jax.random.split(key, 10)
        x = jax.random.normal(ks[0], (B, S, HID), jnp.float32)
        Wq = jax.random.normal(ks[1], (HQ * D, HID), jnp.float32) * 0.02
        Wk = jax.random.normal(ks[2], (HK * D, HID), jnp.float32) * 0.02
        Wv = jax.random.normal(ks[3], (HK * D, HID), jnp.float32) * 0.02
        Wo = jax.random.normal(ks[4], (HID, HQ * D), jnp.float32) * 0.02
        q_norm_w = jax.random.uniform(ks[5], (D,), jnp.float32)
        k_norm_w = jax.random.uniform(ks[6], (D,), jnp.float32)
        k_cache = jax.random.normal(ks[7], (PAGES, PSIZE, HK, D), jnp.float32)
        v_cache = jax.random.normal(ks[8], (PAGES, PSIZE, HK, D), jnp.float32)
        block_table = jnp.arange(B * NPP, dtype=jnp.int32).reshape(B, NPP)
        cache_seqlens = jax.random.randint(ks[9], (B,), 0, 475).astype(jnp.int32)
        return dict(x=x, Wq=Wq, Wk=Wk, Wv=Wv, Wo=Wo, q_norm_w=q_norm_w, k_norm_w=k_norm_w, k_cache=k_cache, v_cache=v_cache, block_table=block_table, cache_seqlens=cache_seqlens)
    _L1_cond_all = _L1_cond_setup()
    _L1_cond_in = {k: v for k, v in _L1_cond_all.items() if k in ('Wq', 'Wk', 'Wv', 'Wo', 'q_norm_w', 'k_norm_w', 'k_cache', 'v_cache')}
    del _L1_cond_all
    return {'x': x, 'itok_B_0_15': itok_B_0_15, 'itok_Bx16_0_63': itok_Bx16_0_63, 'itok_B_207_1644': itok_B_207_1644, 'L0_cond_weight': _L0_cond_in['weight'], 'L1_cond_Wq': _L1_cond_in['Wq'], 'L1_cond_Wk': _L1_cond_in['Wk'], 'L1_cond_Wv': _L1_cond_in['Wv'], 'L1_cond_Wo': _L1_cond_in['Wo'], 'L1_cond_q_norm_w': _L1_cond_in['q_norm_w'], 'L1_cond_k_norm_w': _L1_cond_in['k_norm_w'], 'L1_cond_k_cache': _L1_cond_in['k_cache'], 'L1_cond_v_cache': _L1_cond_in['v_cache']}

def reference(x, itok_B_0_15, itok_Bx16_0_63, itok_B_207_1644, L0_cond_weight, L1_cond_Wq, L1_cond_Wk, L1_cond_Wv, L1_cond_Wo, L1_cond_q_norm_w, L1_cond_k_norm_w, L1_cond_k_cache, L1_cond_v_cache):
    import jax
    import jax.numpy as jnp

    def _L0_cond_ref(x, adapter_ids, weight):
        import jax, jax.numpy as jnp
        import numpy as np
        MAX_LORAS = 16
        IN, OUT = (512, 512)
        B, S = (8, 256)
        w = weight[adapter_ids]
        return jnp.einsum('bsi,boi->bso', x, w)

    def _L1_cond_ref(x, Wq, Wk, Wv, Wo, q_norm_w, k_norm_w, k_cache, v_cache, block_table, cache_seqlens):
        import jax, jax.numpy as jnp
        import numpy as np
        B, S, HID = (4, 128, 512)
        D, HQ, HK = (128, 32, 8)
        PAGES, PSIZE, NPP = (64, 32, 16)
        THETA = 10000.0
        EPS = 1e-06
        SCALE = 1.0 / float(np.sqrt(D))

        def _rmsnorm(t, w):
            var = jnp.mean(t * t, axis=-1, keepdims=True)
            return t * jax.lax.rsqrt(var + EPS) * w

        def _rope(t, pos):
            inv_freq = 1.0 / THETA ** (jnp.arange(0, D, 2, dtype=jnp.float32) / D)
            freqs = pos[..., None].astype(jnp.float32) * inv_freq
            cos = jnp.cos(freqs)[:, :, None, :]
            sin = jnp.sin(freqs)[:, :, None, :]
            t1, t2 = (t[..., :D // 2], t[..., D // 2:])
            return jnp.concatenate([t1 * cos - t2 * sin, t2 * cos + t1 * sin], axis=-1)
        bsz, seqlen, _ = x.shape
        q = jnp.einsum('bsd,ed->bse', x, Wq).reshape(bsz, seqlen, HQ, D)
        k = jnp.einsum('bsd,ed->bse', x, Wk).reshape(bsz, seqlen, HK, D)
        v = jnp.einsum('bsd,ed->bse', x, Wv).reshape(bsz, seqlen, HK, D)
        q = _rmsnorm(q, q_norm_w)
        k = _rmsnorm(k, k_norm_w)
        pos = cache_seqlens[:, None] + jnp.arange(seqlen)[None, :]
        q = _rope(q, pos)
        k = _rope(k, pos)
        L = NPP * PSIZE
        kc = k_cache[block_table].reshape(bsz, L, HK, D)
        vc = v_cache[block_table].reshape(bsz, L, HK, D)
        k_all = jnp.concatenate([kc, k], axis=1)
        v_all = jnp.concatenate([vc, v], axis=1)
        valid_c = jnp.arange(L)[None, :] < cache_seqlens[:, None]
        valid = jnp.concatenate([valid_c, jnp.ones((bsz, seqlen), dtype=bool)], axis=1)
        rep = HQ // HK
        k_all = jnp.repeat(k_all, rep, axis=2)
        v_all = jnp.repeat(v_all, rep, axis=2)
        scores = jnp.einsum('bqhd,bkhd->bhqk', q, k_all) * SCALE
        scores = jnp.where(valid[:, None, None, :], scores, -1e+30)
        probs = jax.nn.softmax(scores, axis=-1)
        o = jnp.einsum('bhqk,bkhd->bqhd', probs, v_all)
        o = o.reshape(bsz, seqlen, HQ * D)
        return jnp.einsum('bse,de->bsd', o, Wo)
    x = x + _L0_cond_ref(x, itok_B_0_15, L0_cond_weight)
    x = x + _L1_cond_ref(x, L1_cond_Wq, L1_cond_Wk, L1_cond_Wv, L1_cond_Wo, L1_cond_q_norm_w, L1_cond_k_norm_w, L1_cond_k_cache, L1_cond_v_cache, itok_Bx16_0_63, itok_B_207_1644)
    return x

_drawn_inputs = setup_inputs


def setup_inputs(seed=0):
    import zlib

    import numpy as np

    out = dict(_drawn_inputs(seed))
    spreads = {}
    factors = {'L1_cond_Wk': 8.0,
     'L1_cond_Wv': 35.381,
     'L1_cond_q_norm_w': 3.166,
     'L1_cond_k_norm_w': 22.24,
     'L1_cond_k_cache': 8.0,
     'L1_cond_v_cache': 8.0}
    for name, (base, spread) in spreads.items():
        noise = np.random.default_rng([zlib.crc32(name.encode()), seed]).standard_normal(out[name].shape)
        drawn = base * np.exp(spread * noise) if base else spread * noise
        out[name] = jnp.asarray(drawn.astype(out[name].dtype))
    for name, factor in factors.items():
        out[name] = (out[name] * factor).astype(out[name].dtype)
    return out
```

```python
from contextlib import ExitStack

import numpy as np

import concourse.bass as bass
from concourse import mybir

F32 = mybir.dt.float32
F32R = mybir.dt.float32r
BF16 = mybir.dt.bfloat16
I32 = mybir.dt.int32
ALU = mybir.AluOpType
ACT = mybir.ActivationFunctionType

P = 128
NB = 8
NK = 8
G = 4
HID = 512
D = 128
NT = 4
KEYS = 640
NU = NB * NK
SCALE = 1.0 / float(np.sqrt(D))
EPS = 1e-6
WC = 1024
NWC = 5
MAGIC = 12582912.0
TWO_PI_1 = 6.28125
TWO_PI_2 = 0.0019350051879882812
TWO_PI_3 = 3.0199159819567027e-07
HALF_PI = 1.5707963267948966
PI_IN = 3.1415925


class Marks:

    def __init__(self):
        self.at = {}
        self.count = {}

    def put(self, name, sem, step):
        assert name not in self.at, name
        self.count[id(sem)] = self.count.get(id(sem), 0) + step
        if name is not None:
            self.at[name] = (sem, self.count[id(sem)])

    def step(self, sem, step):
        self.count[id(sem)] = self.count.get(id(sem), 0) + step


class Queue:

    def __init__(self, marks, sem):
        self.marks, self.sem, self.items = marks, sem, []

    def add(self, fn, name=None, after=()):
        if name is not None:
            self.marks.put(name, self.sem, 1)
        self.items.append((fn, [a for a in after if a is not None], self.sem if name else None, 1))

    def dma(self, fn, sem, name=None, after=()):
        if name is None:
            self.marks.step(sem, 16)
        else:
            self.marks.put(name, sem, 16)
        self.items.append((fn, [a for a in after if a is not None], sem, 16))

    def emit(self, eng):
        seen = {}
        for fn, after, sem, step in self.items:
            for a in after:
                s, v = self.marks.at[a]
                if seen.get(id(s), 0) < v:
                    eng.wait_ge(s, v)
                    seen[id(s)] = v
            ins = fn(eng)
            if sem is not None:
                ins.then_inc(sem, step)


def build(nc, x, xt, lw, wall, kv, ids, table, lens, qw, kw, inv, iota, rows, out):
    with ExitStack() as ctx:
        def sb(name, shape, dt=F32):
            return ctx.enter_context(nc.sbuf_tensor(name, shape, dt))

        def pb(name, shape, dt=F32):
            return ctx.enter_context(nc.psum_tensor(name, shape, dt))

        def sem(name):
            return ctx.enter_context(nc.semaphore(name))

        xh = sb("xh", [P, 4, NB * P], F32R)
        xl = sb("xl", [P, 4, NB * P], F32R)
        acc = sb("acc", [P, NB, HID])
        wh = sb("wh", [P, NWC * WC], F32R)
        wl = sb("wl", [P, NWC * WC], F32R)
        wraw = sb("wraw", [P, 2, WC])
        xts = sb("xts", [P, 2, 4, P])
        lws = sb("lws", [P, 4, HID])
        tab = sb("tab", [P, NB, 4, D])
        mask = sb("mask", [P, NB, KEYS], BF16)
        raw = sb("raw", [P, 2, NT, 2 * D])
        qkv = sb("qkv", [P, 768])
        m1 = sb("m1", [P, G, D])
        m2 = sb("m2", [P, G, D])
        k1 = sb("k1", [P, D])
        k2 = sb("k2", [P, D])
        sqd = sb("sqd", [P, G + 1, D])
        qh = sb("qh", [P, G * P], F32R)
        ql = sb("ql", [P, G * P], F32R)
        kh = sb("kh", [P, KEYS], F32R)
        kl = sb("kl", [P, KEYS], F32R)
        vh = sb("vh", [P, 2, NT + 1, D], F32R)
        vl = sb("vl", [P, 2, NT + 1, D], F32R)
        pr = sb("pr", [P, G, KEYS])
        pth = sb("pth", [P, 3, G * P], F32R)
        ptl = sb("ptl", [P, 3, G * P], F32R)
        oh = sb("oh", [P, G * P], F32R)
        ol = sb("ol", [P, G * P], F32R)
        ident = sb("ident", [P, P])
        ssq = sb("ssq", [P, 2, 8])
        var = sb("var", [P, 2, 8])
        rst = sb("rst", [P, 2, 8])
        mhalf = sb("mhalf", [P, 8])
        mx = sb("mx", [P, 2, G])
        nb = sb("nb", [P, 2, G])
        sm = sb("sm", [P, 2, G])
        rc = sb("rc", [P, 2, G])
        lensb = sb("lensb", [P, NB], I32)
        idsb = sb("idsb", [P, NB], I32)
        tabb = sb("tabb", [P, NB * NT], I32)
        rowsb = sb("rowsb", [P, 4])
        lenf = sb("lenf", [P, NB])
        posf = sb("posf", [P, NB])
        idf = sb("idf", [P, NB])
        tabf = sb("tabf", [P, NB * NT])
        kidx = sb("kidx", [P, NK, NB * NT], I32)
        lidx = sb("lidx", [P, NB, 4], I32)

        inv_s = m1[:, 0, 0:64]
        qw_s = m1[:, 1, :]
        kw_s = m1[:, 2, :]
        ang = pr[:, 0, 0:512].rearrange("p (b f) -> p b f", b=NB)
        rnd = pr[:, 1, 0:512].rearrange("p (b f) -> p b f", b=NB)
        sn = pr[:, 2, 0:512].rearrange("p (b f) -> p b f", b=NB)
        cs = pr[:, 3, 0:512].rearrange("p (b f) -> p b f", b=NB)
        iot = qkv[:, 0:KEYS]

        S = pb("S", [P, 2, 2, 512])
        T = pb("T", [P, 2, 512])
        M = pb("M", [P, 2, 512])

        s_pe, s_act, s_dve, s_pool = sem("s_pe"), sem("s_act"), sem("s_dve"), sem("s_pool")
        d_small = sem("d_small")
        d_w = [sem("d_w0"), sem("d_w1")]
        d_x = [sem("d_x0"), sem("d_x1")]
        d_lw = sem("d_lw")
        d_raw = [sem("d_raw0"), sem("d_raw1")]
        d_out = sem("d_out")

        marks = Marks()
        PE, AC, DV, PO, SP = (Queue(marks, s) for s in (s_pe, s_act, s_dve, s_pool, None))

        def bc(src, n):
            return src.unsqueeze(0).broadcast_to([P, n])

        SP.dma(lambda e: e.dma_start(idsb[:, :], bc(ids, NB)), d_small)
        SP.dma(lambda e: e.dma_start(rowsb[:, :], rows), d_small)
        for g in range(4):
            SP.dma(lambda e, g=g: e.dma_start(
                tabb[32 * g:32 * g + 32, :],
                table[g:g + 1, :].broadcast_to([32, NB * NT])), d_small)
        SP.dma(lambda e: e.dma_start(lensb[:, :], bc(lens, NB)), d_small)
        SP.dma(lambda e: e.dma_start(inv_s, inv), d_small)
        SP.dma(lambda e: e.dma_start(qw_s, bc(qw, D)), d_small)
        SP.dma(lambda e: e.dma_start(kw_s, bc(kw, D)), d_small)
        SP.dma(lambda e: e.dma_start(iot, iota), d_small, "small")

        def load_x(b):
            after = (f"L0mm{b - 2}",) if b >= 2 else ()
            SP.dma(lambda e: e.dma_start(xts[:, b % 2, :, :], xt[b]), d_x[b % 2], after=after)
            SP.dma(lambda e: e.dma_start(acc[:, b, :], x[b]), d_x[b % 2], f"x{b}")

        def load_w(hk, c):
            i = NWC * hk + c
            after = (f"Whi{i - 2}", f"Wlo{i - 2}") if i >= 2 else ()
            SP.dma(lambda e: e.dma_start(wraw[:, i % 2, :], wall[hk, :, c * WC:(c + 1) * WC]),
                   d_w[i % 2], f"W{i}", after)

        PO.add(lambda e: e.memset(ident[:, :], 0.0), "id0")
        PO.add(lambda e: e.affine_select(out=ident[:, :], in_=ident[:, :], compare_op=ALU.not_equal,
                                         fill=1.0, base=0, pattern=[[-1, P]], channel_multiplier=1),
               "ident", ("id0",))
        PO.add(lambda e: e.memset(mhalf[:, :], -0.5), "mhalf")

        DV.add(lambda e: e.tensor_copy(idf[:, :], idsb[:, :]), "idf", ("small",))
        for t in range(4):
            DV.add(lambda e, t=t: e.tensor_scalar(lidx[:, :, t], idf[:, :], 512.0, rowsb[:, 2:3],
                                                  ALU.mult, ALU.add) if t == 0 else
                   e.tensor_scalar(lidx[:, :, t], lidx[:, :, 0], float(128 * t), None, ALU.add),
                   f"lidx{t}", ("idf",) if t == 0 else ("lidx0",))
        DV.add(lambda e: e.tensor_copy(tabf[:, :], tabb[:, :]), "tabf", ("small",))
        DV.add(lambda e: e.tensor_scalar(kidx[:, 0, :], tabf[:, :], 32.0, rowsb[:, 1:2],
                                         ALU.mult, ALU.add), "kidx0", ("tabf",))
        for h in range(1, NK):
            DV.add(lambda e, h=h: e.tensor_scalar(kidx[:, h, :], kidx[:, 0, :], float(2048 * h), None,
                                                  ALU.add), f"kidx{h}", ("kidx0",))
        DV.add(lambda e: e.tensor_copy(lenf[:, :], lensb[:, :]), "lenf", ("small",))
        DV.add(lambda e: e.tensor_scalar(posf[:, :], lenf[:, :], rowsb[:, 0:1], None, ALU.add),
               "posf", ("lenf",))
        for b in range(NB):
            DV.add(lambda e, b=b: e.tensor_scalar(ang[:, b, :], inv_s, posf[:, b:b + 1], None,
                                                  ALU.mult), f"ang{b}", ("posf", "small"))
        DV.add(lambda e: e.tensor_scalar(rnd, ang, float(1.0 / (2 * np.pi)), MAGIC, ALU.mult,
                                         ALU.add), "rnd0", (f"ang{NB - 1}",))
        DV.add(lambda e: e.tensor_scalar(rnd, rnd, -MAGIC, None, ALU.add), "rnd1", ("rnd0",))
        prev = "rnd1"
        for i, c in enumerate((TWO_PI_1, TWO_PI_2, TWO_PI_3)):
            DV.add(lambda e, c=c: e.scalar_tensor_tensor(out=ang, in0=rnd, scalar=-c, in1=ang,
                                                         op0=ALU.mult, op1=ALU.add),
                   f"red{i}", (prev,))
            prev = f"red{i}"
        DV.add(lambda e: e.tensor_scalar(ang, ang, PI_IN, -PI_IN, ALU.min, ALU.max), "red", (prev,))
        DV.add(lambda e: e.tensor_scalar(rnd, ang, -1.0, None, ALU.mult), "neg", ("red",))
        DV.add(lambda e: e.tensor_tensor(rnd, rnd, ang, ALU.max), "abs", ("neg",))
        DV.add(lambda e: e.tensor_scalar(rnd, rnd, -1.0, HALF_PI, ALU.mult, ALU.add), "carg", ("abs",))
        AC.add(lambda e: e.activation(sn, ang, ACT.Sin), "sin", ("red",))
        AC.add(lambda e: e.activation(cs, rnd, ACT.Sin), "cos", ("carg",))
        for b in range(NB):
            DV.add(lambda e, b=b: e.tensor_scalar(mask[:, b, :], iot, lenf[:, b:b + 1], -1e30,
                                                  ALU.is_ge, ALU.mult), f"mask{b}", ("lenf", "small"))

        def halves(ap):
            return ap.rearrange("p (a f) -> p a f", a=2)

        for n, (w, s) in enumerate(((qw_s, SCALE), (kw_s, 1.0))):
            for a in range(2):
                wv = w[:, 64 * a:64 * a + 64].unsqueeze(1).broadcast_to([P, NB, 64])
                DV.add(lambda e, n=n, a=a, wv=wv, s=s: e.scalar_tensor_tensor(
                    out=tab[:, :, 2 * n, 64 * a:64 * a + 64], in0=cs, scalar=s, in1=wv,
                    op0=ALU.mult, op1=ALU.mult), f"tabc{n}{a}", ("cos",))
                DV.add(lambda e, n=n, a=a, wv=wv, s=s: e.scalar_tensor_tensor(
                    out=tab[:, :, 2 * n + 1, 64 * a:64 * a + 64], in0=sn, scalar=-s if a else s,
                    in1=wv, op0=ALU.mult, op1=ALU.mult), f"tabs{n}{a}", ("sin",))

        def if_(cond, name):
            return name if cond else None

        def three(e, o, lh, ll, rh, rl, first, last):
            e.matmul(o, lh, rh, start=first, stop=False)
            e.matmul(o, lh, rl, start=False, stop=False)
            return e.matmul(o, ll, rh, start=False, stop=last)

        def split_w(hk, c, lo_on):
            i = NWC * hk + c
            free = {0: "projq", 1: "projq", 2: "projkv", 3: "y", 4: "y"}[c]
            last = if_(hk > 0, f"{free}{NB * hk - 1}")
            sl = slice(c * WC, (c + 1) * WC)
            AC.add(lambda e: e.activation(wh[:, sl], wraw[:, i % 2, :], ACT.Copy), f"Whi{i}",
                   (f"W{i}", last))
            lo_on.add(lambda e: e.tensor_tensor(wl[:, sl], wraw[:, i % 2, :],
                                                wh[:, sl].bitcast(F32), ALU.subtract),
                      f"Wlo{i}", (f"W{i}", f"Whi{i}", last))

        def gather_l0(b):
            for t in range(4):
                PO.dma(lambda e, t=t: e.indirect_dma_start(
                    out=lws[:, t, :], out_offset=None, in_=lw,
                    in_offset=bass.IndirectOffsetOnAxis(ap=lidx[:, b, t:t + 1], axis=0)),
                    d_lw, f"lw{b}" if t == 3 else None,
                    (f"lidx{t}", if_(b > 0, f"L0mm{b - 1}")))

        def l0_mm(b, free):
            def f(e):
                for t in range(4):
                    i = e.matmul(S[:, 0, 0, :], xts[:, b % 2, t, :], lws[:, t, :],
                                 start=(t == 0), stop=(t == 3))
                return i
            PE.add(f, f"L0mm{b}", (f"x{b}", f"lw{b}", free))

        def l0_add(b):
            DV.add(lambda e: e.tensor_tensor(acc[:, b, :], acc[:, b, :], S[:, 0, 0, :], ALU.add),
                   f"L0add{b}", (f"L0mm{b}", f"x{b}"))

        def l0_t(b, free):
            def f(e):
                for t in range(4):
                    i = e.transpose(S[:, 0, 1, t * P:(t + 1) * P], acc[:, b, t * P:(t + 1) * P],
                                    ident[:, :])
                return i
            PE.add(f, f"L0T{b}", (f"L0add{b}", "ident", free))

        def l0_hi(b):
            src = S[:, 0, 1, :].rearrange("p (t n) -> p t n", t=4)
            AC.add(lambda e: e.activation(xh[:, :, b * P:(b + 1) * P], src, ACT.Copy), f"xh{b}",
                   (f"L0T{b}",))

        def l0_lo(b):
            src = S[:, 0, 1, :].rearrange("p (t n) -> p t n", t=4)
            DV.add(lambda e: e.tensor_tensor(xl[:, :, b * P:(b + 1) * P], src,
                                             xh[:, :, b * P:(b + 1) * P].bitcast(F32), ALU.subtract),
                   f"xl{b}", (f"xh{b}", f"L0T{b}"))

        def gather_kv(v):
            hk, b = divmod(v, NB)
            for t in range(NT):
                PO.dma(lambda e, t=t: e.indirect_dma_start(
                    out=raw[:, v % 2, t, :], out_offset=None, in_=kv,
                    in_offset=bass.IndirectOffsetOnAxis(ap=kidx[:, hk, NT * b + t:NT * b + t + 1],
                                                        axis=0)),
                    d_raw[v % 2], f"raw{v}" if t == NT - 1 else None,
                    (f"kidx{hk}", if_(v >= 2, f"kcT{v - 2}"), if_(v >= 2, f"Vlo{v - 2}")))

        def pe_projq(v):
            hk, b = divmod(v, NB)

            def f(e):
                for t in range(4):
                    xs = slice(b * P, (b + 1) * P)
                    ws = slice(t * 512, (t + 1) * 512)
                    i = three(e, M[:, 0, :], xh[:, t, xs], xl[:, t, xs], wh[:, ws], wl[:, ws],
                              t == 0, t == 3)
                return i
            PE.add(f, f"projq{v}", (f"xl{b}", f"xh{b}", f"Whi{NWC * hk}", f"Whi{NWC * hk + 1}",
                                    f"Wlo{NWC * hk}", f"Wlo{NWC * hk + 1}", if_(v >= 2, f"ol{v - 2}")))

        def pe_projkv(v):
            hk, b = divmod(v, NB)

            def f(e):
                for t in range(4):
                    xs = slice(b * P, (b + 1) * P)
                    ws = slice(2048 + t * 256, 2048 + (t + 1) * 256)
                    i = three(e, M[:, 1, 0:256], xh[:, t, xs], xl[:, t, xs], wh[:, ws], wl[:, ws],
                              t == 0, t == 3)
                return i
            PE.add(f, f"projkv{v}", (f"Whi{NWC * hk + 2}", f"Wlo{NWC * hk + 2}",
                                     if_(v >= 1, f"ql{v - 1}")))

        def pe_kct(v):
            def f(e):
                for t in range(NT):
                    i = e.transpose(T[:, 0, t * P:(t + 1) * P], raw[:, v % 2, t, 0:D], ident[:, :])
                return i
            PE.add(f, f"kcT{v}", (f"raw{v}", "ident", if_(v >= 2, f"ptl{v - 2},4")))

        def pe_knt(v):
            PE.add(lambda e: e.transpose(T[:, 1, 0:P], k1[:, :], ident[:, :]), f"knT{v}",
                   (f"kadd{v}", if_(v >= 2, f"ptl{v - 2},3")))

        def pe_qt(v):
            def f(e):
                for r in range(G):
                    i = e.transpose(M[:, 1, r * P:(r + 1) * P], m1[:, r, :], ident[:, :])
                return i
            PE.add(f, f"qT{v}", (f"qadd{v}", f"copykv{v}"))

        def pe_s(u, g):
            s = g % 2

            def f(e):
                for a in range(2):
                    ks = slice(320 * a, 320 * a + 320)
                    qs = slice(g * P, (g + 1) * P)
                    i = three(e, S[:, s, a, 0:320], qh[:, qs], ql[:, qs], kh[:, ks], kl[:, ks],
                              True, True)
                return i
            prev = f"max{u},{g - 2}" if g >= 2 else if_(u >= 1, f"max{u - 1},{g + 2}")
            l0 = if_(g == 0 and u + 1 < NB, f"xl{u + 1}")
            PE.add(f, f"S{u},{g}", (f"qh{u}", f"ql{u}", f"kch{u}", f"kcl{u}", f"knh{u}", f"knl{u}",
                                    prev, l0))

        def pe_t(u, t):
            def f(e):
                for g in range(G):
                    i = e.transpose(T[:, t % 2, g * P:(g + 1) * P], pr[:, g, t * P:(t + 1) * P],
                                    ident[:, :])
                return i
            if t >= 2:
                free = f"ptl{u},{t - 2}"
            elif u + 1 < NU:
                free = f"kcl{u + 1}" if t == 0 else f"knl{u + 1}"
            else:
                free = f"ptl{u - 1},{4 if t == 0 else 3}"
            PE.add(f, f"T{u},{t}", (f"norm{u},3", free))

        def pe_pv(u, t):
            j = (5 * u + t) % 3
            PE.add(lambda e: three(e, M[:, 0, :], vh[:, u % 2, t, :], vl[:, u % 2, t, :],
                                   pth[:, j, :], ptl[:, j, :], t == 0, t == 4),
                   f"PV{u},{t}", (f"pth{u},{t}", f"ptl{u},{t}", f"Vlo{u}", f"vnl{u}",
                                  if_(u >= 1, f"yadd{u - 1}"), if_(u + 1 < NU, f"copyq{u + 1}")))

        def pe_y(u):
            hk = u // NB

            def f(e):
                for r in range(G):
                    ws = slice(3072 + r * 512, 3072 + (r + 1) * 512)
                    os_ = slice(r * P, (r + 1) * P)
                    i = three(e, M[:, 0, :], oh[:, os_], ol[:, os_], wh[:, ws], wl[:, ws],
                              r == 0, r == 3)
                return i
            PE.add(f, f"y{u}", (f"oh{u}", f"ol{u}", f"Whi{NWC * hk + 3}", f"Whi{NWC * hk + 4}",
                                f"Wlo{NWC * hk + 3}", f"Wlo{NWC * hk + 4}",
                                if_(u + 2 < NU, f"copyq{u + 2}")))

        def ac_copyq(v):
            AC.add(lambda e: e.activation(qkv[:, 0:512], M[:, 0, :], ACT.Copy), f"copyq{v}",
                   (f"projq{v}", if_(v >= 1, f"qm2{v - 1}"),
                    f"mask{NB - 1}" if v == 0 else None))
            for r in range(G):
                AC.add(lambda e, r=r: e.activation(sqd[:, r, :], qkv[:, r * D:(r + 1) * D], ACT.Square,
                                                   accum_out=ssq[:, v % 2, r:r + 1]),
                       f"sq{v},{r}", (f"copyq{v}",))

        def ac_copykv(v):
            AC.add(lambda e: e.activation(qkv[:, 512:768], M[:, 1, 0:256], ACT.Copy), f"copykv{v}",
                   (f"projkv{v}", if_(v >= 1, f"km2{v - 1}"), if_(v >= 1, f"vnl{v - 1}"),
                    f"mask{NB - 1}" if v == 0 else None))
            AC.add(lambda e: e.activation(sqd[:, G, :], qkv[:, 512:640], ACT.Square,
                                          accum_out=ssq[:, v % 2, 4:5]), f"sq{v},4", (f"copykv{v}",))

        def ac_exp(u, g):
            AC.add(lambda e: e.activation(pr[:, g, :], pr[:, g, :], ACT.Exp,
                                          bias=nb[:, u % 2, g:g + 1], scale=rst[:, u % 2, g:g + 1],
                                          accum_out=sm[:, u % 2, g:g + 1]),
                   f"exp{u},{g}", (f"nb{u},{g}", f"rst{u}"))

        def ac_kch(v):
            AC.add(lambda e: e.activation(kh[:, 0:512], T[:, 0, :], ACT.Copy), f"kch{v}",
                   (f"kcT{v}", if_(v >= 1, f"S{v - 1},3")))

        def ac_knh(v):
            AC.add(lambda e: e.activation(kh[:, 512:640], T[:, 1, 0:P], ACT.Copy), f"knh{v}",
                   (f"knT{v}",))

        def ac_qh(v):
            AC.add(lambda e: e.activation(qh[:, :], M[:, 1, :], ACT.Copy), f"qh{v}", (f"qT{v}",))

        def ac_pth(u, t):
            i = 5 * u + t
            j = i % 3
            w = f"PV{(i - 3) // 5},{(i - 3) % 5}" if i >= 3 else None
            AC.add(lambda e: e.activation(pth[:, j, :], T[:, t % 2, :], ACT.Copy), f"pth{u},{t}",
                   (f"T{u},{t}", w))

        def ac_oh(u):
            AC.add(lambda e: e.activation(oh[:, :], M[:, 0, :], ACT.Copy), f"oh{u}",
                   (f"PV{u},4",))

        def dv_max(u, g):
            b = u % NB
            DV.add(lambda e: e.tensor_tensor_reduce(
                pr[:, g, :].rearrange("p (a n) -> p a n", a=2), S[:, g % 2, :, 0:320],
                mask[:, b, :].rearrange("p (a n) -> p a n", a=2), 1.0, -3e38, ALU.add, ALU.max,
                mx[:, u % 2, g:g + 1]), f"max{u},{g}",
                (f"S{u},{g}", f"mask{b}", f"T{u - 1},4" if u else None))
            DV.add(lambda e: e.tensor_scalar(nb[:, u % 2, g:g + 1], mx[:, u % 2, g:g + 1],
                                             rst[:, u % 2, g:g + 1], -1.0, ALU.mult, ALU.mult),
                   f"nb{u},{g}", (f"max{u},{g}", f"rst{u}"))

        def dv_rcp(u, g):
            DV.add(lambda e: e.reciprocal(rc[:, u % 2, g:g + 1], sm[:, u % 2, g:g + 1]),
                   f"rcp{u},{g}", (f"exp{u},{g}",))

        def dv_ropeq(v):
            b = v % NB
            t = qkv[:, 0:512].rearrange("p (r d) -> p r d", r=G)
            c = tab[:, b, 0, :].unsqueeze(1).broadcast_to([P, G, D])
            s = tab[:, b, 1, :].unsqueeze(1).broadcast_to([P, G, D])
            DV.add(lambda e: e.tensor_tensor(m1[:, :, :], t, c, ALU.mult), f"qm1{v}",
                   (f"copyq{v}", if_(v >= 1, f"qT{v - 1}"), "tabc11", "tabs11"))
            DV.add(lambda e: e.tensor_tensor(m2[:, :, :], t, s, ALU.mult), f"qm2{v}",
                   (f"copyq{v}", if_(v >= 1, f"qadd{v - 1}")))

        def dv_ropek(v):
            b = v % NB
            t = qkv[:, 512:640]
            r = rst[:, v % 2, 4:5]
            DV.add(lambda e: e.scalar_tensor_tensor(out=k1[:, :], in0=t, scalar=r, in1=tab[:, b, 2, :],
                                                    op0=ALU.mult, op1=ALU.mult), f"km1{v}",
                   (f"copykv{v}", f"rst{v}", if_(v >= 1, f"knT{v - 1}"), "tabc11", "tabs11"))
            DV.add(lambda e: e.scalar_tensor_tensor(out=k2[:, :], in0=t, scalar=r, in1=tab[:, b, 3, :],
                                                    op0=ALU.mult, op1=ALU.mult), f"km2{v}",
                   (f"copykv{v}", f"rst{v}"))
            DV.add(lambda e: e.tensor_tensor(k1[:, 0:64], k1[:, 0:64], k2[:, 64:128], ALU.add),
                   None, (f"km2{v}",))
            DV.add(lambda e: e.tensor_tensor(k1[:, 64:128], k1[:, 64:128], k2[:, 0:64], ALU.add),
                   f"kadd{v}", (f"km2{v}",))

        def dv_kcl(v):
            DV.add(lambda e: e.tensor_tensor(kl[:, 0:512], T[:, 0, :], kh[:, 0:512].bitcast(F32),
                                             ALU.subtract), f"kcl{v}",
                   (f"kch{v}", if_(v >= 1, f"S{v - 1},3")))

        def dv_knl(v):
            DV.add(lambda e: e.tensor_tensor(kl[:, 512:640], T[:, 1, 0:P],
                                             kh[:, 512:640].bitcast(F32), ALU.subtract),
                   f"knl{v}", (f"knh{v}",))

        def dv_ql(v):
            DV.add(lambda e: e.tensor_tensor(ql[:, :], M[:, 1, :], qh[:, :].bitcast(F32),
                                             ALU.subtract), f"ql{v}", (f"qh{v}",))

        def dv_ptl(u, t):
            j = (5 * u + t) % 3
            DV.add(lambda e: e.tensor_tensor(ptl[:, j, :], T[:, t % 2, :], pth[:, j, :].bitcast(F32),
                                             ALU.subtract), f"ptl{u},{t}", (f"pth{u},{t}",))

        def dv_ol(u):
            DV.add(lambda e: e.tensor_tensor(ol[:, :], M[:, 0, :], oh[:, :].bitcast(F32),
                                             ALU.subtract), f"ol{u}", (f"oh{u}",))

        def dv_yadd(u):
            b = u % NB
            DV.add(lambda e: e.tensor_tensor(acc[:, b, :], acc[:, b, :], M[:, 0, :], ALU.add),
                   f"yadd{u}", (f"y{u}", if_(u < NB, f"L0T{b}")))

        def po_norm(u, g):
            PO.add(lambda e: e.tensor_scalar(pr[:, g, :], pr[:, g, :], rc[:, u % 2, g:g + 1], 1.0,
                                             ALU.mult, ALU.mult), f"norm{u},{g}", (f"rcp{u},{g}",))

        def po_vsplit(v):
            src = raw[:, v % 2, :, D:2 * D]
            war = if_(v >= 2, f"PV{v - 2},4")
            PO.add(lambda e: e.tensor_scalar(vh[:, v % 2, 0:NT, :], src, 1.0, 1.0, ALU.mult,
                                             ALU.mult), f"Vhi{v}", (f"raw{v}", war))
            PO.add(lambda e: e.tensor_tensor(vl[:, v % 2, 0:NT, :], src,
                                             vh[:, v % 2, 0:NT, :].bitcast(F32), ALU.subtract),
                   f"Vlo{v}", (f"Vhi{v}",))

        def po_vnew(v):
            src = qkv[:, 640:768]
            PO.add(lambda e: e.tensor_scalar(vh[:, v % 2, NT, :], src, 1.0, 1.0, ALU.mult,
                                             ALU.mult), f"vnh{v}",
                   (f"copykv{v}", if_(v >= 2, f"PV{v - 2},4")))
            PO.add(lambda e: e.tensor_tensor(vl[:, v % 2, NT, :], src,
                                             vh[:, v % 2, NT, :].bitcast(F32), ALU.subtract),
                   f"vnl{v}", (f"vnh{v}",))

        def po_qadd(v):
            PO.add(lambda e: e.tensor_tensor(m1[:, :, 0:64], m1[:, :, 0:64], m2[:, :, 64:128],
                                             ALU.add), None, (f"qm2{v}",))
            PO.add(lambda e: e.tensor_tensor(m1[:, :, 64:128], m1[:, :, 64:128], m2[:, :, 0:64],
                                             ALU.add), f"qadd{v}", (f"qm2{v}",))

        def po_rst(v):
            s = slice(0, 5)
            PO.add(lambda e: e.tensor_scalar(var[:, v % 2, s], ssq[:, v % 2, s], 1.0 / D, EPS,
                                             ALU.mult, ALU.add), f"var{v}", (f"sq{v},4",))
            PO.add(lambda e: e.tensor_tensor(rst[:, v % 2, s], var[:, v % 2, s], mhalf[:, s],
                                             ALU.pow), f"rst{v}", (f"var{v}", "mhalf"))

        load_x(0)
        load_w(0, 0)
        load_w(0, 1)
        load_x(1)
        gather_l0(0)
        gather_kv(0)
        l0_mm(0, None)
        l0_add(0)
        l0_t(0, None)
        l0_hi(0)
        l0_lo(0)
        gather_l0(1)
        split_w(0, 0, DV)
        split_w(0, 1, PO)
        load_w(0, 2)
        split_w(0, 2, DV)
        load_w(0, 3)
        load_w(0, 4)

        for u in range(-1, NU):
            v = u + 1
            real, nxt = u >= 0, v < NU
            lb = u + 2
            l0 = lb < NB
            hk, b = divmod(u, NB)
            if v + 1 < NU:
                gather_kv(v + 1)
            if real and b == NB - 2 and hk + 1 < NK:
                for c in range(2):
                    load_w(hk + 1, c)
            if real and b == NB - 1 and hk + 1 < NK:
                for c in range(2, 4):
                    load_w(hk + 1, c)
            if real and b == 0 and hk > 0:
                load_w(hk, 4)
            if u >= 1:
                ac_oh(u - 1)
            if real:
                pe_s(u, 0)
                pe_s(u, 1)
                dv_max(u, 0)
                ac_exp(u, 0)
            if u >= 1:
                dv_ol(u - 1)
            if real:
                dv_max(u, 1)
                ac_exp(u, 1)
                dv_rcp(u, 0)
                po_norm(u, 0)
                if b == NB - 1 and hk + 1 < NK:
                    split_w(hk + 1, 0, DV)
                    split_w(hk + 1, 1, DV)
            if nxt:
                pe_projq(v)
                ac_copyq(v)
                po_vsplit(v)
            if real:
                dv_rcp(u, 1)
                po_norm(u, 1)
            if nxt:
                dv_ropeq(v)
                po_qadd(v)
            if real:
                pe_s(u, 2)
                dv_max(u, 2)
                ac_exp(u, 2)
                if b == NB - 1 and hk + 1 < NK:
                    split_w(hk + 1, 2, PO)
            if nxt:
                pe_projkv(v)
                ac_copykv(v)
                po_rst(v)
            if real:
                dv_rcp(u, 2)
                po_norm(u, 2)
                pe_s(u, 3)
                dv_max(u, 3)
                ac_exp(u, 3)
            if nxt:
                pe_kct(v)
                dv_ropek(v)
            if real:
                dv_rcp(u, 3)
                po_norm(u, 3)
            if nxt:
                po_vnew(v)
                ac_kch(v)
                dv_kcl(v)
            if l0:
                l0_mm(lb, f"max{u},2" if real else "xl0")
                l0_add(lb)
                if lb + 1 < NB:
                    gather_l0(lb + 1)
                    load_x(lb + 1)
            if u >= 1:
                pe_y(u - 1)
                dv_yadd(u - 1)
                if u - 1 >= NU - NB:
                    bb = (u - 1) % NB
                    SP.dma(lambda e, bb=bb: e.dma_start(out[bb], acc[:, bb, :]), d_out, f"out{bb}",
                           (f"yadd{u - 1}",))
            if l0:
                l0_t(lb, None)
                l0_hi(lb)
                l0_lo(lb)
            if nxt:
                pe_knt(v)
                pe_qt(v)
                ac_knh(v)
                ac_qh(v)
                dv_knl(v)
                dv_ql(v)
            if real and b == 0:
                split_w(hk, 3, PO)
                split_w(hk, 4, PO)
            if real:
                pe_t(u, 0)
                pe_t(u, 1)
                for t in range(5):
                    pe_pv(u, t)
                    if t + 2 < 5:
                        pe_t(u, t + 2)
                    ac_pth(u, t)
                    dv_ptl(u, t)
        u = NU - 1
        ac_oh(u)
        dv_ol(u)
        pe_y(u)
        dv_yadd(u)
        bb = NB - 1
        SP.dma(lambda e: e.dma_start(out[bb], acc[:, bb, :]), d_out, f"out{bb}", (f"yadd{u}",))

        block = ctx.enter_context(nc.Block())

        @block.sync
        def _(e):
            SP.emit(e)
            e.wait_ge(d_out, 16 * NB)

        @block.gpsimd
        def _(e):
            PO.emit(e)

        @block.scalar
        def _(e):
            AC.emit(e)

        @block.vector
        def _(e):
            DV.emit(e)

        @block.tensor
        def _(e):
            PE.emit(e)


def kernel(x, itok_B_0_15, itok_Bx16_0_63, itok_B_207_1644, L0_cond_weight, L1_cond_Wq, L1_cond_Wk,
           L1_cond_Wv, L1_cond_Wo, L1_cond_q_norm_w, L1_cond_k_norm_w, L1_cond_k_cache,
           L1_cond_v_cache):
    import concourse.bacc as bacc
    from concourse.bass_utils import run_bass_kernel_spmd

    c = np.ascontiguousarray
    x = np.asarray(x)
    wq, wk, wv, wo = (np.asarray(w) for w in (L1_cond_Wq, L1_cond_Wk, L1_cond_Wv, L1_cond_Wo))

    def by_head(w, n):
        return w.reshape(NK, n, 4, P).transpose(0, 3, 2, 1)

    wq_h = by_head(wq, 512).reshape(NK, P, 2048)
    wkv_h = np.concatenate([by_head(wk, 128), by_head(wv, 128)], axis=3).reshape(NK, P, 1024)
    wo_h = wo.reshape(HID, NK, G, D).transpose(1, 3, 2, 0).reshape(NK, P, 2048)
    kc, vc = (np.asarray(a).transpose(2, 0, 1, 3) for a in (L1_cond_k_cache, L1_cond_v_cache))
    inv = (np.float32(1.0) / np.float32(10000.0) ** (np.arange(0, D, 2, dtype=np.float32) /
                                                    np.float32(D))).astype(np.float32)
    iota = np.where(np.arange(KEYS) < 512, np.arange(KEYS), -1.0e9).astype(np.float32)
    p = np.arange(P)
    rows = np.stack([p, p % 32, p, p], axis=1).astype(np.float32)
    arrays = {
        "x": c(x),
        "xt": c(x.reshape(NB, P, 4, P).transpose(0, 3, 2, 1)),
        "lw": c(np.asarray(L0_cond_weight).transpose(0, 2, 1).reshape(16 * HID, HID)),
        "wall": c(np.concatenate([wq_h, wkv_h, wo_h], axis=2)),
        "kv": c(np.stack([kc, vc], axis=3).reshape(NK * 2048, 2 * D)),
        "ids": c(np.asarray(itok_B_0_15)),
        "table": c(np.asarray(itok_Bx16_0_63).reshape(NB * NT, 4).transpose(1, 0)),
        "lens": c(np.asarray(itok_B_207_1644)),
        "qw": c(np.asarray(L1_cond_q_norm_w)),
        "kw": c(np.asarray(L1_cond_k_norm_w)),
        "inv": c(np.broadcast_to(inv, (P, 64))),
        "iota": c(np.broadcast_to(iota, (P, KEYS))),
        "rows": c(rows),
    }
    nc = bacc.Bacc("TRN2", target_bir_lowering=False, num_devices=1)
    ins = {}
    args = []
    for name, a in arrays.items():
        ins[f"in_{name}"] = a
        args.append(nc.dram_tensor(f"in_{name}", a.shape, mybir.dt.from_np(a.dtype),
                                   kind="ExternalInput").ap())
    o = nc.dram_tensor("out_0", (NB, P, HID), F32, kind="ExternalOutput").ap()
    build(nc, *args, o)
    r = run_bass_kernel_spmd(nc, [ins], core_ids=[0])
    return r.results[0]["out_0"]
```

```python
from contextlib import ExitStack

import numpy as np

import concourse.bass as bass
from concourse import mybir

F32 = mybir.dt.float32
F32R = mybir.dt.float32r
BF16 = mybir.dt.bfloat16
I32 = mybir.dt.int32
ALU = mybir.AluOpType
ACT = mybir.ActivationFunctionType

P = 128
NB = 8
NK = 8
G = 4
HID = 512
D = 128
NT = 4
KEYS = 640
NU = NB * NK
SCALE = 1.0 / float(np.sqrt(D))
EPS = 1e-6
WC = 1024
NWC = 5
MAGIC = 12582912.0
TWO_PI_1 = 6.28125
TWO_PI_2 = 0.0019350051879882812
TWO_PI_3 = 3.0199159819567027e-07
HALF_PI = 1.5707963267948966
PI_IN = 3.1415925


class Marks:

    def __init__(self):
        self.at = {}
        self.count = {}

    def put(self, name, sem, step):
        assert name not in self.at, name
        self.count[id(sem)] = self.count.get(id(sem), 0) + step
        if name is not None:
            self.at[name] = (sem, self.count[id(sem)])

    def step(self, sem, step):
        self.count[id(sem)] = self.count.get(id(sem), 0) + step


class Queue:

    def __init__(self, marks, sem):
        self.marks, self.sem, self.items = marks, sem, []

    def add(self, fn, name=None, after=()):
        if name is not None:
            self.marks.put(name, self.sem, 1)
        self.items.append((fn, [a for a in after if a is not None], self.sem if name else None, 1))

    def dma(self, fn, sem, name=None, after=()):
        if name is None:
            self.marks.step(sem, 16)
        else:
            self.marks.put(name, sem, 16)
        self.items.append((fn, [a for a in after if a is not None], sem, 16))

    def emit(self, eng):
        seen = {}
        for fn, after, sem, step in self.items:
            for a in after:
                s, v = self.marks.at[a]
                if seen.get(id(s), 0) < v:
                    eng.wait_ge(s, v)
                    seen[id(s)] = v
            ins = fn(eng)
            if sem is not None:
                ins.then_inc(sem, step)


def build(nc, x, xt, lw, wall, kv, ids, table, lens, qw, kw, inv, iota, rows, out):
    with ExitStack() as ctx:
        def sb(name, shape, dt=F32):
            return ctx.enter_context(nc.sbuf_tensor(name, shape, dt))

        def pb(name, shape, dt=F32):
            return ctx.enter_context(nc.psum_tensor(name, shape, dt))

        def sem(name):
            return ctx.enter_context(nc.semaphore(name))

        xh = sb("xh", [P, 4, NB * P], F32R)
        xl = sb("xl", [P, 4, NB * P], F32R)
        acc = sb("acc", [P, NB, HID])
        wh = sb("wh", [P, NWC * WC], F32R)
        wl = sb("wl", [P, NWC * WC], F32R)
        wraw = sb("wraw", [P, 2, WC])
        xts = sb("xts", [P, 4, P])
        lws = sb("lws", [P, 4, HID])
        tab = sb("tab", [P, NB, 4, D])
        mask = sb("mask", [P, NB, KEYS], BF16)
        raw = sb("raw", [P, 2, NT, 2 * D])
        qkv = sb("qkv", [P, 768])
        m1 = sb("m1", [P, G, D])
        m2 = sb("m2", [P, G, D])
        k1 = sb("k1", [P, D])
        k2 = sb("k2", [P, D])
        sqd = sb("sqd", [P, G + 1, D], BF16)
        qh = sb("qh", [P, G * P], F32R)
        ql = sb("ql", [P, G * P], F32R)
        kh = sb("kh", [P, KEYS], F32R)
        kl = sb("kl", [P, KEYS], F32R)
        vh = sb("vh", [P, 2, NT + 1, D], F32R)
        vl = sb("vl", [P, 2, NT + 1, D], F32R)
        pr = sb("pr", [P, 2, G, KEYS])
        pth = sb("pth", [P, 3, G * P], F32R)
        ptl = sb("ptl", [P, 3, G * P], F32R)
        oh = sb("oh", [P, G * P], F32R)
        ol = sb("ol", [P, G * P], F32R)
        ident = sb("ident", [P, P])
        ssq = sb("ssq", [P, 2, 8])
        var = sb("var", [P, 2, 8])
        rst = sb("rst", [P, 2, 8])
        mhalf = sb("mhalf", [P, 8])
        mx = sb("mx", [P, 2, G])
        nb = sb("nb", [P, 2, G])
        sm = sb("sm", [P, 2, G])
        rc = sb("rc", [P, 2, G])
        lensb = sb("lensb", [P, NB], I32)
        idsb = sb("idsb", [P, NB], I32)
        tabb = sb("tabb", [P, NB * NT], I32)
        rowsb = sb("rowsb", [P, 4])
        lenf = sb("lenf", [P, NB])
        posf = sb("posf", [P, NB])
        idf = sb("idf", [P, NB])
        tabf = sb("tabf", [P, NB * NT])
        kidx = sb("kidx", [P, NK, NB * NT], I32)
        lidx = sb("lidx", [P, NB, 4], I32)

        inv_s = m1[:, 0, 0:64]
        qw_s = m1[:, 1, :]
        kw_s = m1[:, 2, :]
        ang = pr[:, 0, 0, 0:512].rearrange("p (b f) -> p b f", b=NB)
        rnd = pr[:, 0, 1, 0:512].rearrange("p (b f) -> p b f", b=NB)
        sn = pr[:, 0, 2, 0:512].rearrange("p (b f) -> p b f", b=NB)
        cs = pr[:, 0, 3, 0:512].rearrange("p (b f) -> p b f", b=NB)
        iot = qkv[:, 0:KEYS]

        S = pb("S", [P, 2, 2, 512])
        T = pb("T", [P, 2, 512])
        M = pb("M", [P, 2, 512])

        s_pe, s_act, s_dve, s_pool = sem("s_pe"), sem("s_act"), sem("s_dve"), sem("s_pool")
        d_small, d_ids, d_tab = sem("d_small"), sem("d_ids"), sem("d_tab")
        d_w = [sem("d_w0"), sem("d_w1")]
        d_x = [sem("d_x0"), sem("d_x1")]
        d_lw = sem("d_lw")
        d_raw = [sem("d_raw0"), sem("d_raw1")]
        d_out = sem("d_out")

        marks = Marks()
        PE, AC, DV, PO, SP = (Queue(marks, s) for s in (s_pe, s_act, s_dve, s_pool, None))

        t_uses = []
        t_of = {}

        def t_bank(name, evacuated_by):
            t_of[name] = len(t_uses) % 2
            t_uses.append(evacuated_by)
            return t_of[name], t_uses[-3] if len(t_uses) > 2 else None

        def bc(src, n):
            return src.unsqueeze(0).broadcast_to([P, n])

        SP.dma(lambda e: e.dma_start(idsb[:, :], bc(ids, NB)), d_ids)
        AC.dma(lambda e: e.dma_start(rowsb[:, :], rows), d_ids, "ids")
        for g in range(4):
            AC.dma(lambda e, g=g: e.dma_start(
                tabb[32 * g:32 * g + 32, :],
                table[g:g + 1, :].broadcast_to([32, NB * NT])), d_tab, "table" if g == 3 else None)
        AC.dma(lambda e: e.dma_start(lensb[:, :], bc(lens, NB)), d_small)
        AC.dma(lambda e: e.dma_start(inv_s, inv), d_small)
        AC.dma(lambda e: e.dma_start(qw_s, bc(qw, D)), d_small)
        AC.dma(lambda e: e.dma_start(kw_s, bc(kw, D)), d_small)
        AC.dma(lambda e: e.dma_start(iot, iota), d_small, "small")

        def load_x(b):
            after = (f"L0mm{b - 1}",) if b >= 1 else ()
            SP.dma(lambda e: e.dma_start(xts[:, :, :], xt[b]), d_x[b % 2], after=after)
            SP.dma(lambda e: e.dma_start(acc[:, b, :], x[b]), d_x[b % 2], f"x{b}")

        def load_w(hk, c):
            i = NWC * hk + c
            after = (f"Whi{i - 2}", f"Wlo{i - 2}") if i >= 2 else ()
            SP.dma(lambda e: e.dma_start(wraw[:, i % 2, :], wall[hk, :, c * WC:(c + 1) * WC]),
                   d_w[i % 2], f"W{i}", after)

        PO.add(lambda e: e.memset(ident[:, :], 0.0), "id0")
        PO.add(lambda e: e.affine_select(out=ident[:, :], in_=ident[:, :], compare_op=ALU.not_equal,
                                         fill=1.0, base=0, pattern=[[-1, P]], channel_multiplier=1),
               "ident", ("id0",))
        PO.add(lambda e: e.memset(mhalf[:, :], -0.5), "mhalf")

        DV.add(lambda e: e.tensor_copy(idf[:, :], idsb[:, :]), "idf", ("ids",))
        for t in range(4):
            DV.add(lambda e, t=t: e.tensor_scalar(lidx[:, :, t], idf[:, :], 512.0, rowsb[:, 2:3],
                                                  ALU.mult, ALU.add) if t == 0 else
                   e.tensor_scalar(lidx[:, :, t], lidx[:, :, 0], float(128 * t), None, ALU.add),
                   f"lidx{t}", ("idf",) if t == 0 else ("lidx0",))
        DV.add(lambda e: e.tensor_copy(tabf[:, :], tabb[:, :]), "tabf", ("table",))
        DV.add(lambda e: e.tensor_scalar(kidx[:, 0, :], tabf[:, :], 32.0, rowsb[:, 1:2],
                                         ALU.mult, ALU.add), "kidx0", ("tabf", "ids"))
        for h in range(1, NK):
            DV.add(lambda e, h=h: e.tensor_scalar(kidx[:, h, :], kidx[:, 0, :], float(2048 * h), None,
                                                  ALU.add), f"kidx{h}", ("kidx0",))
        DV.add(lambda e: e.tensor_copy(lenf[:, :], lensb[:, :]), "lenf", ("small",))
        DV.add(lambda e: e.tensor_scalar(posf[:, :], lenf[:, :], rowsb[:, 0:1], None, ALU.add),
               "posf", ("lenf",))
        for b in range(NB):
            DV.add(lambda e, b=b: e.tensor_scalar(ang[:, b, :], inv_s, posf[:, b:b + 1], None,
                                                  ALU.mult), f"ang{b}", ("posf", "small"))
        DV.add(lambda e: e.tensor_scalar(rnd, ang, float(1.0 / (2 * np.pi)), MAGIC, ALU.mult,
                                         ALU.add), "rnd0", (f"ang{NB - 1}",))
        DV.add(lambda e: e.tensor_scalar(rnd, rnd, -MAGIC, None, ALU.add), "rnd1", ("rnd0",))
        prev = "rnd1"
        for i, c in enumerate((TWO_PI_1, TWO_PI_2, TWO_PI_3)):
            DV.add(lambda e, c=c: e.scalar_tensor_tensor(out=ang, in0=rnd, scalar=-c, in1=ang,
                                                         op0=ALU.mult, op1=ALU.add),
                   f"red{i}", (prev,))
            prev = f"red{i}"
        DV.add(lambda e: e.tensor_scalar(ang, ang, PI_IN, -PI_IN, ALU.min, ALU.max), "red", (prev,))
        DV.add(lambda e: e.tensor_scalar(rnd, ang, -1.0, None, ALU.mult), "neg", ("red",))
        DV.add(lambda e: e.tensor_tensor(rnd, rnd, ang, ALU.max), "abs", ("neg",))
        DV.add(lambda e: e.tensor_scalar(rnd, rnd, -1.0, HALF_PI, ALU.mult, ALU.add), "carg", ("abs",))
        AC.add(lambda e: e.activation(sn, ang, ACT.Sin), "sin", ("red",))
        AC.add(lambda e: e.activation(cs, rnd, ACT.Sin), "cos", ("carg",))
        for b in range(NB):
            DV.add(lambda e, b=b: e.tensor_scalar(mask[:, b, :], iot, lenf[:, b:b + 1], -1e30,
                                                  ALU.is_ge, ALU.mult), f"mask{b}", ("lenf", "small"))

        def halves(ap):
            return ap.rearrange("p (a f) -> p a f", a=2)

        for n, (w, s) in enumerate(((qw_s, SCALE), (kw_s, 1.0))):
            for a in range(2):
                wv = w[:, 64 * a:64 * a + 64].unsqueeze(1).broadcast_to([P, NB, 64])
                DV.add(lambda e, n=n, a=a, wv=wv, s=s: e.scalar_tensor_tensor(
                    out=tab[:, :, 2 * n, 64 * a:64 * a + 64], in0=cs, scalar=s, in1=wv,
                    op0=ALU.mult, op1=ALU.mult), f"tabc{n}{a}", ("cos",))
                DV.add(lambda e, n=n, a=a, wv=wv, s=s: e.scalar_tensor_tensor(
                    out=tab[:, :, 2 * n + 1, 64 * a:64 * a + 64], in0=sn, scalar=-s if a else s,
                    in1=wv, op0=ALU.mult, op1=ALU.mult), f"tabs{n}{a}", ("sin",))

        def if_(cond, name):
            return name if cond else None

        def three(e, o, lh, ll, rh, rl, first, last):
            e.matmul(o, lh, rh, start=first, stop=False)
            e.matmul(o, lh, rl, start=False, stop=False)
            return e.matmul(o, ll, rh, start=False, stop=last)

        def split_w(hk, c, lo_on):
            i = NWC * hk + c
            free = {0: "projq", 1: "projq", 2: "projkv", 3: "y", 4: "y"}[c]
            last = if_(hk > 0, f"{free}{NB * hk - 1}")
            sl = slice(c * WC, (c + 1) * WC)
            AC.add(lambda e: e.activation(wh[:, sl], wraw[:, i % 2, :], ACT.Copy), f"Whi{i}",
                   (f"W{i}", last))
            lo_on.add(lambda e: e.tensor_tensor(wl[:, sl], wraw[:, i % 2, :],
                                                wh[:, sl].bitcast(F32), ALU.subtract),
                      f"Wlo{i}", (f"W{i}", f"Whi{i}", last))

        def gather_l0(b):
            for t in range(4):
                PO.dma(lambda e, t=t: e.indirect_dma_start(
                    out=lws[:, t, :], out_offset=None, in_=lw,
                    in_offset=bass.IndirectOffsetOnAxis(ap=lidx[:, b, t:t + 1], axis=0)),
                    d_lw, f"lw{b}" if t == 3 else None,
                    (f"lidx{t}", if_(b > 0, f"L0mm{b - 1}")))

        def l0_mm(b, free):
            def f(e):
                for t in range(4):
                    i = e.matmul(S[:, 0, 0, :], xts[:, t, :], lws[:, t, :],
                                 start=(t == 0), stop=(t == 3))
                return i
            PE.add(f, f"L0mm{b}", (f"x{b}", f"lw{b}", free))

        def l0_add(b):
            DV.add(lambda e: e.tensor_tensor(acc[:, b, :], acc[:, b, :], S[:, 0, 0, :], ALU.add),
                   f"L0add{b}", (f"L0mm{b}", f"x{b}"))

        def l0_t(b, free):
            def f(e):
                for t in range(4):
                    i = e.transpose(S[:, 0, 1, t * P:(t + 1) * P], acc[:, b, t * P:(t + 1) * P],
                                    ident[:, :])
                return i
            PE.add(f, f"L0T{b}", (f"L0add{b}", "ident", free))

        def l0_hi(b):
            src = S[:, 0, 1, :].rearrange("p (t n) -> p t n", t=4)
            AC.add(lambda e: e.activation(xh[:, :, b * P:(b + 1) * P], src, ACT.Copy), f"xh{b}",
                   (f"L0T{b}",))

        def l0_lo(b):
            src = S[:, 0, 1, :].rearrange("p (t n) -> p t n", t=4)
            DV.add(lambda e: e.tensor_tensor(xl[:, :, b * P:(b + 1) * P], src,
                                             xh[:, :, b * P:(b + 1) * P].bitcast(F32), ALU.subtract),
                   f"xl{b}", (f"xh{b}", f"L0T{b}"))

        def gather_kv(v, t):
            hk, b = divmod(v, NB)
            PO.dma(lambda e: e.indirect_dma_start(
                out=raw[:, v % 2, t, :], out_offset=None, in_=kv,
                in_offset=bass.IndirectOffsetOnAxis(ap=kidx[:, hk, NT * b + t:NT * b + t + 1],
                                                    axis=0)),
                d_raw[v % 2], f"raw{v}" if t == NT - 1 else None,
                (f"kidx{hk}", if_(v >= 2, f"kcT{v - 2}"), if_(v >= 2, f"Vlo{v - 2}")))

        def pe_projq(v):
            hk, b = divmod(v, NB)

            def f(e):
                for t in range(4):
                    xs = slice(b * P, (b + 1) * P)
                    ws = slice(t * 512, (t + 1) * 512)
                    i = three(e, M[:, 0, :], xh[:, t, xs], xl[:, t, xs], wh[:, ws], wl[:, ws],
                              t == 0, t == 3)
                return i
            PE.add(f, f"projq{v}", (f"xl{b}", f"xh{b}", f"Whi{NWC * hk}", f"Whi{NWC * hk + 1}",
                                    f"Wlo{NWC * hk}", f"Wlo{NWC * hk + 1}", if_(v >= 2, f"ol{v - 2}")))

        def pe_projkv(v):
            hk, b = divmod(v, NB)

            def f(e):
                for t in range(4):
                    xs = slice(b * P, (b + 1) * P)
                    ws = slice(2048 + t * 256, 2048 + (t + 1) * 256)
                    i = three(e, M[:, 1, 0:256], xh[:, t, xs], xl[:, t, xs], wh[:, ws], wl[:, ws],
                              t == 0, t == 3)
                return i
            PE.add(f, f"projkv{v}", (f"Whi{NWC * hk + 2}", f"Wlo{NWC * hk + 2}",
                                     if_(v >= 3, f"yadd{v - 3}")))

        def pe_kct(v):
            k, free = t_bank(f"kcT{v}", f"kcl{v}")

            def f(e):
                for t in range(NT):
                    i = e.transpose(T[:, k, t * P:(t + 1) * P], raw[:, v % 2, t, 0:D], ident[:, :])
                return i
            PE.add(f, f"kcT{v}", (f"raw{v}", "ident", free))

        def pe_knt(v):
            k, free = t_bank(f"knT{v}", f"knl{v}")
            PE.add(lambda e: e.transpose(T[:, k, 0:P], k1[:, :], ident[:, :]), f"knT{v}",
                   (f"kadd{v}", free))

        def pe_qt(v):
            def f(e):
                for r in range(G):
                    i = e.transpose(M[:, 0, r * P:(r + 1) * P], m1[:, r, :], ident[:, :])
                return i
            PE.add(f, f"qT{v}", (f"qadd{v}", f"copyq{v}"))

        def pe_s(u, g):
            s = g % 2
            qs = slice(g * P, (g + 1) * P)

            def part(l, r, first, last):
                def f(e):
                    for a in range(2):
                        i = e.matmul(S[:, s, a, 0:320], l[:, qs], r[:, 320 * a:320 * a + 320],
                                     start=first, stop=last)
                    return i
                return f
            prev = f"max{u},{g - 2}" if g >= 2 else if_(u >= 1, f"max{u - 1},{g + 2}")
            l0 = if_(g == 0 and u + 1 < NB, f"xl{u + 1}")
            PE.add(part(qh, kh, True, False), None, (f"qh{u}", f"kch{u}", f"knh{u}", prev, l0))
            PE.add(part(qh, kl, False, False), None, (f"kcl{u}", f"knl{u}"))
            PE.add(part(ql, kh, False, True), f"S{u},{g}", (f"ql{u}",))

        def pe_t(u, t):
            k, free = t_bank(f"T{u},{t}", f"ptl{u},{t}")

            def f(e):
                for g in range(G):
                    i = e.transpose(T[:, k, g * P:(g + 1) * P],
                                    pr[:, u % 2, g, t * P:(t + 1) * P], ident[:, :])
                return i
            PE.add(f, f"T{u},{t}", (f"norm{u},3", free))

        def pe_pv(u, t):
            j = (5 * u + t) % 3
            PE.add(lambda e: three(e, M[:, 0, :], vh[:, u % 2, t, :], vl[:, u % 2, t, :],
                                   pth[:, j, :], ptl[:, j, :], t == 0, t == 4),
                   f"PV{u},{t}", (f"pth{u},{t}", f"ptl{u},{t}", f"Vlo{u}", f"vnl{u}",
                                  if_(u + 1 < NU, f"ql{u + 1}")))

        def pe_y(u):
            hk = u // NB

            def f(e):
                for r in range(G):
                    ws = slice(3072 + r * 512, 3072 + (r + 1) * 512)
                    os_ = slice(r * P, (r + 1) * P)
                    i = three(e, M[:, 1, :], oh[:, os_], ol[:, os_], wh[:, ws], wl[:, ws],
                              r == 0, r == 3)
                return i
            PE.add(f, f"y{u}", (f"oh{u}", f"ol{u}", f"Whi{NWC * hk + 3}", f"Whi{NWC * hk + 4}",
                                f"Wlo{NWC * hk + 3}", f"Wlo{NWC * hk + 4}",
                                if_(u + 2 < NU, f"copyq{u + 2}")))

        def ac_copyq(v):
            AC.add(lambda e: e.activation(qkv[:, 0:512], M[:, 0, :], ACT.Copy), f"copyq{v}",
                   (f"projq{v}", if_(v >= 1, f"qm2{v - 1}"),
                    f"mask{NB - 1}" if v == 0 else None))
            for r in range(G):
                AC.add(lambda e, r=r: e.activation(sqd[:, r, :], qkv[:, r * D:(r + 1) * D], ACT.Square,
                                                   accum_out=ssq[:, v % 2, r:r + 1]),
                       f"sq{v},{r}", (f"copyq{v}",))

        def ac_copykv(v):
            AC.add(lambda e: e.activation(qkv[:, 512:768], M[:, 1, 0:256], ACT.Copy), f"copykv{v}",
                   (f"projkv{v}", if_(v >= 1, f"km2{v - 1}"), if_(v >= 1, f"vnl{v - 1}"),
                    f"mask{NB - 1}" if v == 0 else None))
            AC.add(lambda e: e.activation(sqd[:, G, :], qkv[:, 512:640], ACT.Square,
                                          accum_out=ssq[:, v % 2, 4:5]), f"sq{v},4", (f"copykv{v}",))

        def ac_exp(u, g):
            AC.add(lambda e: e.activation(pr[:, u % 2, g, :], pr[:, u % 2, g, :], ACT.Exp,
                                          bias=nb[:, u % 2, g:g + 1], scale=rst[:, u % 2, g:g + 1],
                                          accum_out=sm[:, u % 2, g:g + 1]),
                   f"exp{u},{g}", (f"nb{u},{g}", f"rstq{u}"))

        def ac_kch(v):
            AC.add(lambda e: e.activation(kh[:, 0:512], T[:, t_of[f"kcT{v}"], :], ACT.Copy), f"kch{v}",
                   (f"kcT{v}", if_(v >= 1, f"S{v - 1},3")))

        def ac_knh(v):
            AC.add(lambda e: e.activation(kh[:, 512:640], T[:, t_of[f"knT{v}"], 0:P], ACT.Copy), f"knh{v}",
                   (f"knT{v}",))

        def ac_qh(v):
            AC.add(lambda e: e.activation(qh[:, :], M[:, 0, :], ACT.Copy), f"qh{v}", (f"qT{v}", if_(v >= 1, f"S{v - 1},3")))

        def ac_pth(u, t):
            i = 5 * u + t
            j = i % 3
            w = f"PV{(i - 3) // 5},{(i - 3) % 5}" if i >= 3 else None
            AC.add(lambda e: e.activation(pth[:, j, :], T[:, t_of[f"T{u},{t}"], :], ACT.Copy), f"pth{u},{t}",
                   (f"T{u},{t}", w))

        def ac_oh(u):
            AC.add(lambda e: e.activation(oh[:, :], M[:, 0, :], ACT.Copy), f"oh{u}",
                   (f"PV{u},4",))

        def dv_max(u, g):
            b = u % NB
            DV.add(lambda e: e.tensor_tensor_reduce(
                pr[:, u % 2, g, :].rearrange("p (a n) -> p a n", a=2), S[:, g % 2, :, 0:320],
                mask[:, b, :].rearrange("p (a n) -> p a n", a=2), 1.0, -3e38, ALU.add, ALU.max,
                mx[:, u % 2, g:g + 1]), f"max{u},{g}",
                (f"S{u},{g}", f"mask{b}", if_(u >= 2, f"T{u - 2},4"), "tabs11" if u == 0 else None))
            DV.add(lambda e: e.tensor_scalar(nb[:, u % 2, g:g + 1], mx[:, u % 2, g:g + 1],
                                             rst[:, u % 2, g:g + 1], -1.0, ALU.mult, ALU.mult),
                   f"nb{u},{g}", (f"max{u},{g}", f"rstq{u}"))

        def dv_rcp(u, g):
            DV.add(lambda e: e.reciprocal(rc[:, u % 2, g:g + 1], sm[:, u % 2, g:g + 1]),
                   f"rcp{u},{g}", (f"exp{u},{g}",))

        def dv_ropeq(v):
            b = v % NB
            t = qkv[:, 0:512].rearrange("p (r d) -> p r d", r=G)
            c = tab[:, b, 0, :].unsqueeze(1).broadcast_to([P, G, D])
            s = tab[:, b, 1, :].unsqueeze(1).broadcast_to([P, G, D])
            DV.add(lambda e: e.tensor_tensor(m1[:, :, :], t, c, ALU.mult), f"qm1{v}",
                   (f"copyq{v}", if_(v >= 1, f"qT{v - 1}"), "tabc11", "tabs11"))
            DV.add(lambda e: e.tensor_tensor(m2[:, :, :], t, s, ALU.mult), f"qm2{v}",
                   (f"copyq{v}", if_(v >= 1, f"qadd{v - 1}")))

        def dv_qadd(v):
            DV.add(lambda e: e.tensor_tensor(m1[:, :, 0:64], m1[:, :, 0:64], m2[:, :, 64:128],
                                             ALU.add), None, (f"qm2{v}",))
            DV.add(lambda e: e.tensor_tensor(m1[:, :, 64:128], m1[:, :, 64:128], m2[:, :, 0:64],
                                             ALU.add), f"qadd{v}", (f"qm2{v}",))

        def dv_ropek(v):
            b = v % NB
            t = qkv[:, 512:640]
            r = rst[:, v % 2, 4:5]
            DV.add(lambda e: e.scalar_tensor_tensor(out=k1[:, :], in0=t, scalar=r, in1=tab[:, b, 2, :],
                                                    op0=ALU.mult, op1=ALU.mult), f"km1{v}",
                   (f"copykv{v}", f"rstk{v}", if_(v >= 1, f"knT{v - 1}"), "tabc11", "tabs11"))
            DV.add(lambda e: e.scalar_tensor_tensor(out=k2[:, :], in0=t, scalar=r, in1=tab[:, b, 3, :],
                                                    op0=ALU.mult, op1=ALU.mult), f"km2{v}",
                   (f"copykv{v}", f"rstk{v}"))
            DV.add(lambda e: e.tensor_tensor(k1[:, 0:64], k1[:, 0:64], k2[:, 64:128], ALU.add),
                   None, (f"km2{v}",))
            DV.add(lambda e: e.tensor_tensor(k1[:, 64:128], k1[:, 64:128], k2[:, 0:64], ALU.add),
                   f"kadd{v}", (f"km2{v}",))

        def dv_kcl(v):
            DV.add(lambda e: e.tensor_tensor(kl[:, 0:512], T[:, t_of[f"kcT{v}"], :], kh[:, 0:512].bitcast(F32),
                                             ALU.subtract), f"kcl{v}",
                   (f"kch{v}", if_(v >= 1, f"S{v - 1},3")))

        def dv_knl(v):
            DV.add(lambda e: e.tensor_tensor(kl[:, 512:640], T[:, t_of[f"knT{v}"], 0:P],
                                             kh[:, 512:640].bitcast(F32), ALU.subtract),
                   f"knl{v}", (f"knh{v}",))

        def dv_ql(v):
            DV.add(lambda e: e.tensor_tensor(ql[:, :], M[:, 0, :], qh[:, :].bitcast(F32),
                                             ALU.subtract), f"ql{v}", (f"qh{v}",))

        def dv_ptl(u, t):
            j = (5 * u + t) % 3
            DV.add(lambda e: e.tensor_tensor(ptl[:, j, :], T[:, t_of[f"T{u},{t}"], :], pth[:, j, :].bitcast(F32),
                                             ALU.subtract), f"ptl{u},{t}", (f"pth{u},{t}",))

        def dv_ol(u):
            DV.add(lambda e: e.tensor_tensor(ol[:, :], M[:, 0, :], oh[:, :].bitcast(F32),
                                             ALU.subtract), f"ol{u}", (f"oh{u}",))

        def dv_yadd(u):
            b = u % NB
            DV.add(lambda e: e.tensor_tensor(acc[:, b, :], acc[:, b, :], M[:, 1, :], ALU.add),
                   f"yadd{u}", (f"y{u}", if_(u < NB, f"L0T{b}")))

        def po_norm(u, g):
            PO.add(lambda e: e.tensor_scalar(pr[:, u % 2, g, :], pr[:, u % 2, g, :], rc[:, u % 2, g:g + 1], 1.0,
                                             ALU.mult, ALU.mult), f"norm{u},{g}", (f"rcp{u},{g}",))

        def po_vsplit(v):
            src = raw[:, v % 2, :, D:2 * D]
            war = if_(v >= 2, f"PV{v - 2},4")
            PO.add(lambda e: e.tensor_scalar(vh[:, v % 2, 0:NT, :], src, 1.0, 1.0, ALU.mult,
                                             ALU.mult), f"Vhi{v}", (f"raw{v}", war))
            PO.add(lambda e: e.tensor_tensor(vl[:, v % 2, 0:NT, :], src,
                                             vh[:, v % 2, 0:NT, :].bitcast(F32), ALU.subtract),
                   f"Vlo{v}", (f"Vhi{v}",))

        def po_vnew(v):
            src = qkv[:, 640:768]
            PO.add(lambda e: e.tensor_scalar(vh[:, v % 2, NT, :], src, 1.0, 1.0, ALU.mult,
                                             ALU.mult), f"vnh{v}",
                   (f"copykv{v}", if_(v >= 2, f"PV{v - 2},4")))
            PO.add(lambda e: e.tensor_tensor(vl[:, v % 2, NT, :], src,
                                             vh[:, v % 2, NT, :].bitcast(F32), ALU.subtract),
                   f"vnl{v}", (f"vnh{v}",))

        def po_rst(v, part):
            s = slice(4, 5) if part == "k" else slice(0, 4)
            last = f"sq{v},4" if part == "k" else f"sq{v},3"
            PO.add(lambda e: e.tensor_scalar(var[:, v % 2, s], ssq[:, v % 2, s], 1.0 / D, EPS,
                                             ALU.mult, ALU.add), f"var{part}{v}", (last,))
            PO.add(lambda e: e.tensor_tensor(rst[:, v % 2, s], var[:, v % 2, s], mhalf[:, s],
                                             ALU.pow), f"rst{part}{v}", (f"var{part}{v}", "mhalf"))

        load_x(0)
        load_w(0, 0)
        load_w(0, 1)
        load_x(1)
        gather_l0(0)
        for t in range(NT):
            gather_kv(0, t)
        l0_mm(0, None)
        l0_add(0)
        l0_t(0, None)
        l0_hi(0)
        l0_lo(0)
        gather_l0(1)
        split_w(0, 0, DV)
        split_w(0, 1, PO)
        load_w(0, 2)
        split_w(0, 2, DV)
        load_w(0, 3)
        load_w(0, 4)

        for u in range(-1, NU + 1):
            v, w = u + 1, u - 1
            real, nxt, old = 0 <= u < NU, v < NU, w >= 0
            lb = u + 2
            l0 = lb < NB
            hk, b = divmod(u, NB)
            more = hk + 1 < NK
            if real and b == NB - 2 and more:
                for c in range(NWC):
                    load_w(hk + 1, c)
            for g in range(G + 1):
                if real and g < G:
                    pe_s(u, g)
                if old:
                    if g + 2 < 5:
                        pe_t(w, g + 2)
                    pe_pv(w, g)
                if real and g < G:
                    dv_max(u, g)
                if old and g + 2 < 5:
                    ac_pth(w, g + 2)
                    dv_ptl(w, g + 2)
                if real and g < G:
                    ac_exp(u, g)
                    if g >= 1:
                        dv_rcp(u, g - 1)
                        po_norm(u, g - 1)
                if v + 1 < NU and g < NT:
                    gather_kv(v + 1, g)
                if real and b == NB - 1 and more and g in (0, 2):
                    split_w(hk + 1, 1 + g // 2, DV)
            if old:
                ac_oh(w)
                dv_ol(w)
            if nxt:
                pe_projkv(v)
                ac_copykv(v)
            if real:
                dv_rcp(u, 3)
                po_norm(u, 3)
            if nxt:
                pe_kct(v)
                pe_projq(v)
                po_rst(v, "k")
                po_vnew(v)
                dv_ropek(v)
                ac_copyq(v)
                dv_ropeq(v)
                dv_qadd(v)
                po_rst(v, "q")
                po_vsplit(v)
                ac_kch(v)
                dv_kcl(v)
            if l0:
                l0_mm(lb, f"max{u},2" if real else "xl0")
                l0_add(lb)
                if lb + 1 < NB:
                    gather_l0(lb + 1)
                    load_x(lb + 1)
            if old:
                pe_y(w)
                dv_yadd(w)
                if w >= NU - NB:
                    bb = w % NB
                    SP.dma(lambda e, bb=bb: e.dma_start(out[bb], acc[:, bb, :]), d_out, f"out{bb}",
                           (f"yadd{w}",))
            if l0:
                l0_t(lb, None)
                l0_hi(lb)
                l0_lo(lb)
            if nxt:
                pe_knt(v)
                pe_qt(v)
                ac_knh(v)
                ac_qh(v)
                dv_knl(v)
                dv_ql(v)
            if real:
                pe_t(u, 0)
                pe_t(u, 1)
                for t in range(2):
                    ac_pth(u, t)
                    dv_ptl(u, t)
            if real and b == NB - 2 and more:
                split_w(hk + 1, 0, DV)
            if real and b == 0:
                split_w(hk, 3, DV)
                split_w(hk, 4, DV)

        block = ctx.enter_context(nc.Block())

        @block.sync
        def _(e):
            SP.emit(e)
            e.wait_ge(d_out, 16 * NB)

        @block.gpsimd
        def _(e):
            PO.emit(e)

        @block.scalar
        def _(e):
            AC.emit(e)

        @block.vector
        def _(e):
            DV.emit(e)

        @block.tensor
        def _(e):
            PE.emit(e)


def kernel(x, itok_B_0_15, itok_Bx16_0_63, itok_B_207_1644, L0_cond_weight, L1_cond_Wq, L1_cond_Wk,
           L1_cond_Wv, L1_cond_Wo, L1_cond_q_norm_w, L1_cond_k_norm_w, L1_cond_k_cache,
           L1_cond_v_cache):
    import concourse.bacc as bacc
    from concourse.bass_utils import run_bass_kernel_spmd

    c = np.ascontiguousarray
    x = np.asarray(x)
    wq, wk, wv, wo = (np.asarray(w) for w in (L1_cond_Wq, L1_cond_Wk, L1_cond_Wv, L1_cond_Wo))

    def by_head(w, n):
        return w.reshape(NK, n, 4, P).transpose(0, 3, 2, 1)

    wq_h = by_head(wq, 512).reshape(NK, P, 2048)
    wkv_h = np.concatenate([by_head(wk, 128), by_head(wv, 128)], axis=3).reshape(NK, P, 1024)
    wo_h = wo.reshape(HID, NK, G, D).transpose(1, 3, 2, 0).reshape(NK, P, 2048)
    kc, vc = (np.asarray(a).transpose(2, 0, 1, 3) for a in (L1_cond_k_cache, L1_cond_v_cache))
    inv = (np.float32(1.0) / np.float32(10000.0) ** (np.arange(0, D, 2, dtype=np.float32) /
                                                    np.float32(D))).astype(np.float32)
    iota = np.where(np.arange(KEYS) < 512, np.arange(KEYS), -1.0e9).astype(np.float32)
    p = np.arange(P)
    rows = np.stack([p, p % 32, p, p], axis=1).astype(np.float32)
    arrays = {
        "x": c(x),
        "xt": c(x.reshape(NB, P, 4, P).transpose(0, 3, 2, 1)),
        "lw": c(np.asarray(L0_cond_weight).transpose(0, 2, 1).reshape(16 * HID, HID)),
        "wall": c(np.concatenate([wq_h, wkv_h, wo_h], axis=2)),
        "kv": c(np.stack([kc, vc], axis=3).reshape(NK * 2048, 2 * D)),
        "ids": c(np.asarray(itok_B_0_15)),
        "table": c(np.asarray(itok_Bx16_0_63).reshape(NB * NT, 4).transpose(1, 0)),
        "lens": c(np.asarray(itok_B_207_1644)),
        "qw": c(np.asarray(L1_cond_q_norm_w)),
        "kw": c(np.asarray(L1_cond_k_norm_w)),
        "inv": c(np.broadcast_to(inv, (P, 64))),
        "iota": c(np.broadcast_to(iota, (P, KEYS))),
        "rows": c(rows),
    }
    nc = bacc.Bacc("TRN2", target_bir_lowering=False, num_devices=1)
    ins = {}
    args = []
    for name, a in arrays.items():
        ins[f"in_{name}"] = a
        args.append(nc.dram_tensor(f"in_{name}", a.shape, mybir.dt.from_np(a.dtype),
                                   kind="ExternalInput").ap())
    o = nc.dram_tensor("out_0", (NB, P, HID), F32, kind="ExternalOutput").ap()
    build(nc, *args, o)
    r = run_bass_kernel_spmd(nc, [ins], core_ids=[0])
    return r.results[0]["out_0"]
```

```python
from contextlib import ExitStack

import numpy as np

import concourse.bass as bass
from concourse import mybir

F32 = mybir.dt.float32
F32R = mybir.dt.float32r
BF16 = mybir.dt.bfloat16
I32 = mybir.dt.int32
ALU = mybir.AluOpType
ACT = mybir.ActivationFunctionType

P = 128
NB = 8
NK = 8
G = 4
HID = 512
D = 128
NT = 4
NPG = 16
PSZ = 32
KEYS = 640
NU = NB * NK
SCALE = 1.0 / float(np.sqrt(D))
EPS = 1e-6
WC = 512
NWC = 10
NWR = 4
N_WARM = 30
MAGIC = 12582912.0
TWO_PI_1 = 6.28125
TWO_PI_2 = 0.0019350051879882812
TWO_PI_3 = 3.0199159819567027e-07
HALF_PI = 1.5707963267948966
PI_IN = 3.1415925


SPLITS = (
    ("lo", 0, 6, 2, "dve"),
    ("lo", 1, 6, 3, "dve"),
    ("lo", 2, 6, 5, "dve"),
    ("lo", 3, 7, 0, "dve"),
    ("lo", 4, 7, 1, "dve"),
    ("lo", 5, 7, 3, "dve"),
    ("lo", 6, 1, 0, "dve"),
    ("lo", 7, 1, 1, "dve"),
    ("lo", 8, 1, 1, "pool"),
    ("lo", 9, 1, 3, "dve"),
    ("hi", 0, 6, 1, "act"),
    ("hi", 1, 6, 2, "act"),
    ("hi", 2, 6, 4, "pool"),
    ("hi", 3, 6, 5, "act"),
    ("hi", 4, 7, 0, "act"),
    ("hi", 5, 7, 2, "act"),
    ("hi", 6, 0, 5, "pool"),
    ("hi", 7, 1, 0, "act"),
    ("hi", 8, 1, 0, "pool"),
    ("hi", 9, 1, 2, "act"),
)


class Marks:

    def __init__(self):
        self.at = {}
        self.count = {}

    def put(self, name, sem, step):
        assert name not in self.at, name
        self.count[id(sem)] = self.count.get(id(sem), 0) + step
        if name is not None:
            self.at[name] = (sem, self.count[id(sem)])

    def step(self, sem, step):
        self.count[id(sem)] = self.count.get(id(sem), 0) + step


class Queue:

    def __init__(self, marks, sem):
        self.marks, self.sem, self.items = marks, sem, []

    def add(self, fn, name=None, after=()):
        if name is not None:
            self.marks.put(name, self.sem, 1)
        self.items.append((fn, [a for a in after if a is not None], self.sem if name else None, 1))

    def dma(self, fn, sem, name=None, after=()):
        if name is None:
            self.marks.step(sem, 16)
        else:
            self.marks.put(name, sem, 16)
        self.items.append((fn, [a for a in after if a is not None], sem, 16))

    def emit(self, eng):
        seen = {}
        for fn, after, sem, step in self.items:
            for a in after:
                s, v = self.marks.at[a]
                if seen.get(id(s), 0) < v:
                    eng.wait_ge(s, v)
                    seen[id(s)] = v
            ins = fn(eng)
            if sem is not None:
                ins.then_inc(sem, step)


def build(nc, x, xt, lw, wall, kt, vrows, ids_lens, table, pages, qkw, consts, iota, out):
    with ExitStack() as ctx:
        def sb(name, shape, dt=F32):
            return ctx.enter_context(nc.sbuf_tensor(name, shape, dt))

        def pb(name, shape, dt=F32):
            return ctx.enter_context(nc.psum_tensor(name, shape, dt))

        def sem(name):
            return ctx.enter_context(nc.semaphore(name))

        xh = sb("xh", [P, 4, NB * P], F32R)
        xl = sb("xl", [P, 4, NB * P], F32R)
        acc = sb("acc", [P, NB, HID])
        wh = sb("wh", [P, NWC * WC], F32R)
        wl = sb("wl", [P, NWC * WC], F32R)
        wraw = sb("wraw", [P, NWR, WC])
        xts = sb("xts", [P, 4, P])
        lws = sb("lws", [P, 4, HID])
        tab = sb("tab", [P, NB, 4, D])
        mask = sb("mask", [P, NB, KEYS], BF16)
        rawk = sb("rawk", [P, 2, NT * P])
        rawv = sb("rawv", [P, 2, NT, D])
        qkv = sb("qkv", [P, 768])
        m1 = sb("m1", [P, G, D])
        m2 = sb("m2", [P, G, D])
        k1 = sb("k1", [P, D])
        k2 = sb("k2", [P, D])
        sqd = sb("sqd", [P, G + 1, D], BF16)
        qh = sb("qh", [P, G * P], F32R)
        ql = sb("ql", [P, G * P], F32R)
        kh = sb("kh", [P, KEYS], F32R)
        kl = sb("kl", [P, KEYS], F32R)
        vh = sb("vh", [P, 2, NT + 1, D], F32R)
        vl = sb("vl", [P, 2, NT + 1, D], F32R)
        pr = sb("pr", [P, 2, G, KEYS])
        pth = sb("pth", [P, 3, G * P], F32R)
        ptl = sb("ptl", [P, 3, G * P], F32R)
        oh = sb("oh", [P, G * P], F32R)
        ol = sb("ol", [P, G * P], F32R)
        ident = sb("ident", [P, P])
        ssq = sb("ssq", [P, 2, 8])
        var = sb("var", [P, 2, 8])
        rst = sb("rst", [P, 2, 8])
        mhalf = sb("mhalf", [P, 8])
        warmed = sb("warmed", [P, 8])
        mx = sb("mx", [P, 2, G])
        nb = sb("nb", [P, 2, G])
        sm = sb("sm", [P, 2, G])
        rc = sb("rc", [P, 2, G])
        il = sb("il", [P, 2 * NB], I32)
        tabb = sb("tabb", [P, NB * NT], I32)
        page = sb("page", [1, NB * NPG], I32)
        cst = sb("cst", [P, 3 + 64])
        rowsb = cst[:, 0:3]
        ilf = sb("ilf", [P, 2 * NB])
        idf = ilf[:, 0:NB]
        lenf = ilf[:, NB:2 * NB]
        posf = sb("posf", [P, NB])
        tabf = sb("tabf", [P, NB * NT])
        kidx = sb("kidx", [P, 2, NB * NT], I32)
        lidx = sb("lidx", [P, NB, 4], I32)

        inv_s = cst[:, 3:67]
        qkw_s = sb("qkw_s", [P, 2 * D])[:, :]
        qw_s, kw_s = qkw_s[:, 0:D], qkw_s[:, D:2 * D]
        ang = pr[:, 0, 0, 0:512].rearrange("p (b f) -> p b f", b=NB)
        rnd = pr[:, 0, 1, 0:512].rearrange("p (b f) -> p b f", b=NB)
        sn = acc[:, NB - 2, :].rearrange("p (b f) -> p b f", b=NB)
        cs = acc[:, NB - 3, :].rearrange("p (b f) -> p b f", b=NB)
        iot = acc[:, NB - 1, :]
        lws1 = pr[:, 1, :, :].rearrange("p g k -> p (g k)")[:, 0:2048].rearrange("p (t n) -> p t n", t=4)
        xts1 = pr[:, 1, :, :].rearrange("p g k -> p (g k)")[:, 2048:2560].rearrange(
            "p (t n) -> p t n", t=4)

        S = pb("S", [P, 2, 2, 512])
        T = pb("T", [P, 2, 512])
        M = pb("M", [P, 2, 512])

        s_pe, s_act, s_dve, s_pool = sem("s_pe"), sem("s_act"), sem("s_dve"), sem("s_pool")
        d_small, d_ids, d_tab = sem("d_small"), sem("d_ids"), sem("d_tab")
        d_w = [sem(f"d_w{i}") for i in range(NWR)]
        d_x = [sem("d_x0"), sem("d_x1")]
        d_lw = [[sem(f"d_lw{b}{t}") for t in range(4)] for b in range(2)]
        d_iota = sem("d_iota")
        d_rawk = [sem("d_rawk0"), sem("d_rawk1")]
        d_rawv = [sem("d_rawv0"), sem("d_rawv1")]
        d_page = sem("d_page")
        d_out = sem("d_out")

        kt_regs = [nc.sync.alloc_register(f"page{j}") for j in range(4)]

        marks = Marks()
        PE, AC, DV, PO, SP = (Queue(marks, s) for s in (s_pe, s_act, s_dve, s_pool, None))

        t_uses = []
        t_of = {}

        def t_bank(name, evacuated_by):
            t_of[name] = len(t_uses) % 2
            t_uses.append(evacuated_by)
            return t_of[name], t_uses[-3] if len(t_uses) > 2 else None

        def bc(src, n):
            return src.unsqueeze(0).broadcast_to([P, n])

        SP.dma(lambda e: e.dma_start(il[:, :], bc(ids_lens, 2 * NB)), d_ids)
        AC.dma(lambda e: e.dma_start(cst[:, :], consts), d_ids, "ids")
        AC.dma(lambda e: e.dma_start(page[:, :], pages), d_page, "page")
        AC.dma(lambda e: e.dma_start(qkw_s, bc(qkw, 2 * D)), d_small, "small")
        for g in range(4):
            AC.dma(lambda e, g=g: e.dma_start(
                tabb[32 * g:32 * g + 32, :],
                table[g:g + 1, :].broadcast_to([32, NB * NT])), d_tab, "table" if g == 3 else None)

        AC.dma(lambda e: e.dma_start(iot, iota), d_iota, "iota")

        def load_x(b):
            dst = xts1 if b == 1 else xts[:, :, :]
            last = {0: None, 1: None, 2: "L0mm0"}.get(b, f"L0mm{b - 1}")
            SP.dma(lambda e: e.dma_start(dst, xt[b]), d_x[b % 2], after=(last,))
            SP.dma(lambda e: e.dma_start(acc[:, b, :], x[b]), d_x[b % 2], f"x{b}",
                   ("mask7",) if b == NB - 1 else ("rope131",) if b >= NB - 3 else ())

        def load_w(hk, c):
            i = NWC * hk + c
            after = (f"Whi{i - NWR}", f"Wlo{i - NWR}") if i >= NWR else ()
            SP.dma(lambda e: e.dma_start(wraw[:, i % NWR, :], wall[hk, :, c * WC:(c + 1) * WC]),
                   d_w[i % NWR], f"W{i}", after)

        PO.add(lambda e: e.memset(ident[:, :], 0.0), "id0")
        PO.add(lambda e: e.affine_select(out=ident[:, :], in_=ident[:, :], compare_op=ALU.not_equal,
                                         fill=1.0, base=0, pattern=[[-1, P]], channel_multiplier=1),
               "ident", ("id0",))
        PO.add(lambda e: e.memset(mhalf[:, :], -0.5), "mhalf")

        PO.add(lambda e: e.memset(mask[:, :, 512:KEYS], 0.0), "mask_new")

        DV.add(lambda e: e.tensor_copy(ilf[:, :], il[:, :]), "ilf", ("ids",))
        DV.add(lambda e: e.tensor_scalar(lidx[:, :, 0], idf, 512.0, rowsb[:, 0:1],
                                         ALU.mult, ALU.add), "lidx0", ("ilf",))
        for t in range(1, 4):
            DV.add(lambda e, t=t: e.tensor_scalar(lidx[:, :, t], lidx[:, :, 0], float(128 * t), None,
                                                  ALU.add), f"lidx{t}", ("lidx0",))
        def key_rows(heads):
            for h in heads:
                if h == 0:
                    DV.add(lambda e: e.tensor_copy(tabf[:, :], tabb[:, :]), "tabf", ("table",))
                    DV.add(lambda e: e.tensor_scalar(kidx[:, 0, :], tabf[:, :], 32.0, rowsb[:, 1:2],
                                                     ALU.mult, ALU.add), "kidx0", ("tabf", "ids"))
                else:
                    last = f"rawv{NB * (h - 1) - 1}" if h >= 2 else None
                    DV.add(lambda e, h=h: e.tensor_scalar(kidx[:, h % 2, :], kidx[:, (h - 1) % 2, :],
                                                          2048.0, None, ALU.add),
                           f"kidx{h}", (f"kidx{h - 1}", last))

        def angles():
            DV.add(lambda e: e.tensor_scalar(posf[:, :], lenf, rowsb[:, 0:1], None, ALU.add),
                   "posf", ("ilf",))
            for b in range(NB):
                DV.add(lambda e, b=b: e.tensor_scalar(ang[:, b, :], inv_s, posf[:, b:b + 1], None,
                                                      ALU.mult), f"ang{b}", ("posf", "ids"))
            DV.add(lambda e: e.tensor_scalar(rnd, ang, float(1.0 / (2 * np.pi)), MAGIC, ALU.mult,
                                             ALU.add), "rnd0", (f"ang{NB - 1}",))
            DV.add(lambda e: e.tensor_scalar(rnd, rnd, -MAGIC, None, ALU.add), "rnd1", ("rnd0",))
            prev = "rnd1"
            for i, c in enumerate((TWO_PI_1, TWO_PI_2, TWO_PI_3)):
                DV.add(lambda e, c=c: e.scalar_tensor_tensor(out=ang, in0=rnd, scalar=-c, in1=ang,
                                                             op0=ALU.mult, op1=ALU.add),
                       f"red{i}", (prev,))
                prev = f"red{i}"
            DV.add(lambda e: e.tensor_scalar(ang, ang, PI_IN, -PI_IN, ALU.min, ALU.max), "red",
                   (prev,))
            DV.add(lambda e: e.scalar_tensor_tensor(out=rnd, in0=ang, scalar=-1.0, in1=ang,
                                                    op0=ALU.mult, op1=ALU.max), "abs", ("red",))
            DV.add(lambda e: e.tensor_scalar(rnd, rnd, -1.0, HALF_PI, ALU.mult, ALU.add), "carg",
                   ("abs",))

        def warm(func, after):
            AC.add(lambda e: e.activation(warmed[:, :], mhalf[:, :], func), None, after)

        def warm_pe(e):
            for _ in range(N_WARM):
                i = e.transpose(T[:, 1, 0:P], ident[:, :], ident[:, :])
            return i

        def sines():
            AC.add(lambda e: e.activation(sn, ang, ACT.Sin), "sin", ("red",))
            AC.add(lambda e: e.activation(cs, rnd, ACT.Sin), "cos", ("carg",))

        def masks(bs):
            for b in bs:
                DV.add(lambda e, b=b: e.tensor_scalar(mask[:, b, 0:512], iot, lenf[:, b:b + 1], -1e30,
                                                      ALU.is_ge, ALU.mult), f"mask{b}",
                       ("ilf", "iota", "mask_new"))

        def rope_table(n, part, rest, on=DV):
            w, c = ((qw_s, SCALE), (kw_s, 1.0))[n]
            bs = slice(2, NB) if rest else slice(0, 2)
            a, sine = part % 2, part < 2
            src = sn if sine else cs
            wv = w[:, 64 * a:64 * a + 64].unsqueeze(1).broadcast_to([P, NB - 2 if rest else 2, 64])
            dst = tab[:, bs, 2 * n + (1 if sine else 0), 64 * a:64 * a + 64]
            k = -c if sine and a else c
            name, after = f"rope{n}{part}{rest}", ("sin" if sine else "cos", "small")
            if on is DV:
                DV.add(lambda e: e.scalar_tensor_tensor(out=dst, in0=src[:, bs, :], scalar=k,
                                                        in1=wv, op0=ALU.mult, op1=ALU.mult),
                       name, after)
            else:
                PO.add(lambda e: e.tensor_tensor(dst, src[:, bs, :], wv, ALU.mult),
                       name + "w", after)
                PO.add(lambda e: e.tensor_scalar(dst, dst, k, 1.0, ALU.mult, ALU.mult), name,
                       (name + "w",))

        def if_(cond, name):
            return name if cond else None

        def three(e, o, lh, ll, rh, rl, first, last):
            e.matmul(o, lh, rh, start=first, stop=False)
            e.matmul(o, lh, rl, start=False, stop=False)
            return e.matmul(o, ll, rh, start=False, stop=last)

        def last_use(u, c):
            return f"projq{u},{c}" if c < 4 else f"projkv{u}" if c < 6 else f"y{u},{(c - 6) // 2}"

        def split_hi(hk, c, on="act"):
            i = NWC * hk + c
            last = last_use(NB * hk - 1, c) if hk > 0 else None
            sl = slice(c * WC, (c + 1) * WC)
            if on == "act":
                AC.add(lambda e: e.activation(wh[:, sl], wraw[:, i % NWR, :], ACT.Copy),
                       f"Whi{i}", (f"W{i}", last))
            else:
                PO.add(lambda e: e.tensor_scalar(wh[:, sl], wraw[:, i % NWR, :], 1.0, 1.0,
                                                 ALU.mult, ALU.mult), f"Whi{i}", (f"W{i}", last))

        def split_lo(hk, c, on="dve"):
            i = NWC * hk + c
            sl = slice(c * WC, (c + 1) * WC)
            q = DV if on == "dve" else PO
            q.add(lambda e: e.tensor_tensor(wl[:, sl], wraw[:, i % NWR, :],
                                            wh[:, sl].bitcast(F32), ALU.subtract),
                  f"Wlo{i}", (f"W{i}", f"Whi{i}"))
            if c + NWR < NWC:
                load_w(hk, c + NWR)

        def gather_l0(b):
            dst = lws1 if b == 1 else lws
            last = {0: None, 1: None, 2: "L0mm0"}.get(b, f"L0mm{b - 1}")
            for t in range(4):
                PO.dma(lambda e, t=t: e.indirect_dma_start(
                    out=dst[:, t, :], out_offset=None, in_=lw,
                    in_offset=bass.IndirectOffsetOnAxis(ap=lidx[:, b, t:t + 1], axis=0)),
                    d_lw[b % 2][t], f"lw{b},{t}", (f"lidx{t}", last))

        def l0_banks(b):
            if b == 1:
                return M[:, 0, :], T[:, 0, :]
            return S[:, 0, 0, :], S[:, 0, 1, :] if b == 0 else M[:, 0, :]

        def l0_mm(b, free):
            xs, ws = (xts1, lws1) if b == 1 else (xts, lws)
            for t in range(4):
                PE.add(lambda e, t=t: e.matmul(l0_banks(b)[0], xs[:, t, :], ws[:, t, :],
                                               start=(t == 0), stop=(t == 3)),
                       f"L0mm{b}" if t == 3 else None, (f"x{b}", f"lw{b},{t}", free))

        def l0_add(b):
            DV.add(lambda e: e.tensor_tensor(acc[:, b, :], acc[:, b, :], l0_banks(b)[0], ALU.add),
                   f"L0add{b}", (f"L0mm{b}", f"x{b}"))

        def l0_t(b, free):
            def f(e):
                for t in range(4):
                    i = e.transpose(l0_banks(b)[1][:, t * P:(t + 1) * P],
                                    acc[:, b, t * P:(t + 1) * P], ident[:, :])
                return i
            PE.add(f, f"L0T{b}", (f"L0add{b}", "ident", free))

        def l0_hi(b):
            src = l0_banks(b)[1].rearrange("p (t n) -> p t n", t=4)
            AC.add(lambda e: e.activation(xh[:, :, b * P:(b + 1) * P], src, ACT.Copy), f"xh{b}",
                   (f"L0T{b}",))

        def l0_lo(b):
            src = l0_banks(b)[1].rearrange("p (t n) -> p t n", t=4)
            DV.add(lambda e: e.tensor_tensor(xl[:, :, b * P:(b + 1) * P], src,
                                             xh[:, :, b * P:(b + 1) * P].bitcast(F32), ALU.subtract),
                   f"xl{b}", (f"xh{b}", f"L0T{b}"))

        def gather_v(v, t):
            hk, b = divmod(v, NB)
            PO.dma(lambda e: e.indirect_dma_start(
                out=rawv[:, v % 2, t, :], out_offset=None, in_=vrows,
                in_offset=bass.IndirectOffsetOnAxis(ap=kidx[:, hk % 2, NT * b + t:NT * b + t + 1],
                                                    axis=0)),
                d_rawv[v % 2], f"rawv{v}" if t == NT - 1 else None,
                (f"kidx{hk}", if_(v >= 2, f"Vlo{v - 2}")))

        def load_kt(v, t):
            hk, b = divmod(v, NB)
            numbers = []

            for j in range(4):
                def f(e, j=j):
                    if j == 0:
                        first = NPG * b + 4 * t
                        e.load(kt_regs, page[0:1, first:first + 4])
                        numbers.extend(e.snap(r, min_val=0, max_val=63) for r in kt_regs)
                    k = 4 * t + j
                    return e.dma_start(
                        rawk[:, v % 2, k * PSZ:(k + 1) * PSZ],
                        kt[hk, bass.ds(numbers[j], 1), :, :].rearrange("a p n -> (a p) n"))
                SP.dma(f, d_rawk[v % 2], f"rawk{v}" if 4 * t + j == NPG - 1 else None,
                       ("page", if_(v >= 2, f"kcl{v - 2}")))

        def pe_projq(v, t):
            hk, b = divmod(v, NB)
            xs = slice(b * P, (b + 1) * P)
            ws = slice(t * 512, (t + 1) * 512)
            i = NWC * hk + t
            PE.add(lambda e: three(e, M[:, 1, :], xh[:, t, xs], xl[:, t, xs], wh[:, ws], wl[:, ws],
                                   t == 0, t == 3), f"projq{v},{t}",
                   (f"xh{b}", f"xl{b}", f"Whi{i}", f"Wlo{i}", if_(v >= 1, f"ql{v - 1}")))

        def kv_bank(v):
            return M[:, 1, 0:256] if v else S[:, 1, 0, 0:256]

        def pe_projkv(v):
            hk, b = divmod(v, NB)
            xs = slice(b * P, (b + 1) * P)

            def f(e):
                for t in range(4):
                    ws = slice(2048 + t * 256, 2048 + (t + 1) * 256)
                    i = three(e, kv_bank(v), xh[:, t, xs], xl[:, t, xs], wh[:, ws], wl[:, ws],
                              t == 0, t == 3)
                return i
            i = NWC * hk + 4
            PE.add(f, f"projkv{v}", (f"Whi{i}", f"Wlo{i}", f"Whi{i + 1}", f"Wlo{i + 1}",
                                     f"copyq{v}" if v else None))

        def pe_knt(v):
            PE.add(lambda e: e.transpose(S[:, 1, 1, 0:P], k1[:, :], ident[:, :]), f"knT{v}",
                   (f"kadd{v}", if_(v >= 1, f"max{v - 1},3")))

        def pe_qt(v):
            def f(e):
                for r in range(G):
                    i = e.transpose(M[:, 1, r * P:(r + 1) * P], m1[:, r, :], ident[:, :])
                return i
            PE.add(f, f"qT{v}", (f"qadd{v}", f"copykv{v}" if v else None))

        def pe_s(u, g):
            s = g % 2
            qs = slice(g * P, (g + 1) * P)

            def part(l, r, first, last):
                def f(e):
                    for a in range(2):
                        i = e.matmul(S[:, s, a, 0:320], l[:, qs], r[:, 320 * a:320 * a + 320],
                                     start=first, stop=last)
                    return i
                return f
            prev = f"max{u},{g - 2}" if g >= 2 else if_(u >= 1, f"max{u - 1},{g + 2}")
            l0 = if_(g == 0 and 1 <= u and u + 1 < NB, f"L0add{u + 1}")
            y = if_(g == 1 and u != 1, f"yadd{u - 2}" if u else "copykv0")
            PE.add(part(qh, kh, True, False), None, (f"qh{u}", f"kch{u}", f"knh{u}", prev, l0, y))
            PE.add(part(qh, kl, False, False), None, (f"kcl{u}", f"knl{u}"))
            PE.add(part(ql, kh, False, True), f"S{u},{g}", (f"ql{u}",))

        def pe_t(u, t):
            k, free = t_bank(f"T{u},{t}", f"ptl{u},{t}")

            def f(e):
                for g in range(G):
                    i = e.transpose(T[:, k, g * P:(g + 1) * P],
                                    pr[:, u % 2, g, t * P:(t + 1) * P], ident[:, :])
                return i
            PE.add(f, f"T{u},{t}", (f"norm{u},3", free, "xl1" if u == 0 and t == 0 else None))

        def pe_pv(u, t):
            j = (5 * u + t) % 3
            PE.add(lambda e: three(e, M[:, 0, :], vh[:, u % 2, t, :], vl[:, u % 2, t, :],
                                   pth[:, j, :], ptl[:, j, :], t == 0, t == 4),
                   f"PV{u},{t}", (f"pth{u},{t}", f"ptl{u},{t}", f"Vlo{u}", f"vnl{u}",
                                  f"ol{u - 1}" if u >= 1 else "L0add1",
                                  f"xl{u + 2}" if t == 0 and u + 2 < NB else None))

        def pe_y(u, half):
            hk = u // NB

            def part(l, rs, first, last):
                def f(e):
                    for r in (2 * half, 2 * half + 1):
                        os_ = slice(r * P, (r + 1) * P)
                        ws = slice(3072 + r * 512, 3072 + (r + 1) * 512)
                        for w in rs:
                            i = e.matmul(S[:, 1, 0, :], l[:, os_], w[:, ws],
                                         start=(first and r == 0 and w is wh),
                                         stop=(last and r == 3))
                    return i
                return f
            i = NWC * hk + 6 + 2 * half
            free = f"max{u + 1},3" if u + 1 < NU else f"yadd{u - 1}"
            PE.add(part(oh, (wh, wl), half == 0, False), None,
                   (f"oh{u}", f"Whi{i}", f"Wlo{i}", f"Whi{i + 1}", f"Wlo{i + 1}", free))
            PE.add(part(ol, (wh,), False, half == 1), f"y{u},{half}", (f"ol{u}",))

        def ac_copyq(v):
            AC.add(lambda e: e.activation(qkv[:, 0:512], M[:, 1, :], ACT.Copy), f"copyq{v}",
                   (f"projq{v},3", if_(v >= 1, f"qm2{v - 1}"),))

        def ac_sqq(v):
            for r in range(G):
                AC.add(lambda e, r=r: e.activation(sqd[:, r, :], qkv[:, r * D:(r + 1) * D], ACT.Square,
                                                   accum_out=ssq[:, v % 2, r:r + 1]),
                       f"sq{v},{r}", (f"copyq{v}",))

        def ac_copykv(v):
            AC.add(lambda e: e.activation(qkv[:, 512:768], kv_bank(v), ACT.Copy), f"copykv{v}",
                   (f"projkv{v}", if_(v >= 1, f"km2{v - 1}"), if_(v >= 1, f"vnl{v - 1}"),))
            AC.add(lambda e: e.activation(sqd[:, G, :], qkv[:, 512:640], ACT.Square,
                                          accum_out=ssq[:, v % 2, 4:5]), f"sq{v},4", (f"copykv{v}",))

        def ac_exp(u, g):
            AC.add(lambda e: e.activation(pr[:, u % 2, g, :], pr[:, u % 2, g, :], ACT.Exp,
                                          bias=nb[:, u % 2, g:g + 1], scale=rst[:, u % 2, g:g + 1],
                                          accum_out=sm[:, u % 2, g:g + 1]),
                   f"exp{u},{g}", (f"nb{u},{g}", f"rstq{u}"))

        def ac_kch(v):
            AC.add(lambda e: e.activation(kh[:, 0:512], rawk[:, v % 2, :], ACT.Copy), f"kch{v}",
                   (f"rawk{v}", if_(v >= 1, f"S{v - 1},3")))

        def ac_knh(v):
            AC.add(lambda e: e.activation(kh[:, 512:640], S[:, 1, 1, 0:P], ACT.Copy), f"knh{v}",
                   (f"knT{v}",))

        def ac_qh(v):
            AC.add(lambda e: e.activation(qh[:, :], M[:, 1, :], ACT.Copy), f"qh{v}", (f"qT{v}", if_(v >= 1, f"S{v - 1},3")))

        def ac_pth(u, t):
            i = 5 * u + t
            j = i % 3
            w = f"PV{(i - 3) // 5},{(i - 3) % 5}" if i >= 3 else None
            AC.add(lambda e: e.activation(pth[:, j, :], T[:, t_of[f"T{u},{t}"], :], ACT.Copy), f"pth{u},{t}",
                   (f"T{u},{t}", w))

        def ac_oh(u):
            AC.add(lambda e: e.activation(oh[:, :], M[:, 0, :], ACT.Copy), f"oh{u}",
                   (f"PV{u},4",))

        def dv_max(u, g):
            b = u % NB
            DV.add(lambda e: e.tensor_tensor_reduce(
                pr[:, u % 2, g, :].rearrange("p (a n) -> p a n", a=2), S[:, g % 2, :, 0:320],
                mask[:, b, :].rearrange("p (a n) -> p a n", a=2), 1.0, -3e38, ALU.add, ALU.max,
                mx[:, u % 2, g:g + 1]), f"max{u},{g}",
                (f"S{u},{g}", f"mask{b}", f"T{u - 2},4" if u >= 2 else "L0mm1" if u == 1 else "cos"))
            DV.add(lambda e: e.tensor_scalar(nb[:, u % 2, g:g + 1], mx[:, u % 2, g:g + 1],
                                             rst[:, u % 2, g:g + 1], -1.0, ALU.mult, ALU.mult),
                   f"nb{u},{g}", (f"max{u},{g}", f"rstq{u}"))

        def dv_rcp(u, g):
            DV.add(lambda e: e.reciprocal(rc[:, u % 2, g:g + 1], sm[:, u % 2, g:g + 1]),
                   f"rcp{u},{g}", (f"exp{u},{g}",))

        def dv_ropeq(v):
            b = v % NB
            t = qkv[:, 0:512].rearrange("p (r d) -> p r d", r=G)
            c = tab[:, b, 0, :].unsqueeze(1).broadcast_to([P, G, D])
            DV.add(lambda e: e.tensor_tensor(m1[:, :, :], t, c, ALU.mult), f"qm1{v}",
                   (f"copyq{v}", if_(v >= 1, f"qT{v - 1}"), "rope030" if v < 2 else "rope031"))

        def dv_ropeq2(v):
            b = v % NB
            t = qkv[:, 0:512].rearrange("p (r d) -> p r d", r=G)
            s = tab[:, b, 1, :].unsqueeze(1).broadcast_to([P, G, D])
            DV.add(lambda e: e.tensor_tensor(m2[:, :, :], t, s, ALU.mult), f"qm2{v}",
                   (f"copyq{v}", if_(v >= 1, f"qadd{v - 1}")))

        def dv_qadd(v):
            DV.add(lambda e: e.tensor_tensor(m1[:, :, 0:64], m1[:, :, 0:64], m2[:, :, 64:128],
                                             ALU.add), None, (f"qm2{v}",))
            DV.add(lambda e: e.tensor_tensor(m1[:, :, 64:128], m1[:, :, 64:128], m2[:, :, 0:64],
                                             ALU.add), f"qadd{v}", (f"qm2{v}",))

        def dv_ropek(v):
            b = v % NB
            t = qkv[:, 512:640]
            r = rst[:, v % 2, 4:5]
            DV.add(lambda e: e.scalar_tensor_tensor(out=k1[:, :], in0=t, scalar=r, in1=tab[:, b, 2, :],
                                                    op0=ALU.mult, op1=ALU.mult), f"km1{v}",
                   (f"copykv{v}", f"rstk{v}", if_(v >= 1, f"knT{v - 1}"),
                    "rope130" if v < 2 else "rope131"))
            DV.add(lambda e: e.scalar_tensor_tensor(out=k2[:, :], in0=t, scalar=r, in1=tab[:, b, 3, :],
                                                    op0=ALU.mult, op1=ALU.mult), f"km2{v}",
                   (f"copykv{v}", f"rstk{v}"))
            DV.add(lambda e: e.tensor_tensor(k1[:, 0:64], k1[:, 0:64], k2[:, 64:128], ALU.add),
                   None, (f"km2{v}",))
            DV.add(lambda e: e.tensor_tensor(k1[:, 64:128], k1[:, 64:128], k2[:, 0:64], ALU.add),
                   f"kadd{v}", (f"km2{v}",))

        def dv_kcl(v):
            DV.add(lambda e: e.tensor_tensor(kl[:, 0:512], rawk[:, v % 2, :], kh[:, 0:512].bitcast(F32),
                                             ALU.subtract), f"kcl{v}",
                   (f"kch{v}", if_(v >= 1, f"S{v - 1},3")))

        def dv_knl(v):
            DV.add(lambda e: e.tensor_tensor(kl[:, 512:640], S[:, 1, 1, 0:P],
                                             kh[:, 512:640].bitcast(F32), ALU.subtract),
                   f"knl{v}", (f"knh{v}",))

        def dv_ql(v):
            DV.add(lambda e: e.tensor_tensor(ql[:, :], M[:, 1, :], qh[:, :].bitcast(F32),
                                             ALU.subtract), f"ql{v}", (f"qh{v}",))

        def dv_ptl(u, t):
            j = (5 * u + t) % 3
            DV.add(lambda e: e.tensor_tensor(ptl[:, j, :], T[:, t_of[f"T{u},{t}"], :], pth[:, j, :].bitcast(F32),
                                             ALU.subtract), f"ptl{u},{t}", (f"pth{u},{t}",))

        def dv_ol(u):
            DV.add(lambda e: e.tensor_tensor(ol[:, :], M[:, 0, :], oh[:, :].bitcast(F32),
                                             ALU.subtract), f"ol{u}", (f"oh{u}",))

        def dv_yadd(u):
            b = u % NB
            DV.add(lambda e: e.tensor_tensor(acc[:, b, :], acc[:, b, :], S[:, 1, 0, :], ALU.add),
                   f"yadd{u}", (f"y{u},1", if_(u < NB, f"L0T{b}")))

        def po_norm(u, g):
            PO.add(lambda e: e.tensor_scalar(pr[:, u % 2, g, :], pr[:, u % 2, g, :], rc[:, u % 2, g:g + 1], 1.0,
                                             ALU.mult, ALU.mult), f"norm{u},{g}", (f"rcp{u},{g}",))

        def po_vsplit(v, part):
            src = rawv[:, v % 2, :, :]
            if part == "hi":
                PO.add(lambda e: e.tensor_scalar(vh[:, v % 2, 0:NT, :], src, 1.0, 1.0, ALU.mult,
                                                 ALU.mult), f"Vhi{v}",
                       (f"rawv{v}", if_(v >= 2, f"PV{v - 2},4")))
            else:
                PO.add(lambda e: e.tensor_tensor(vl[:, v % 2, 0:NT, :], src,
                                                 vh[:, v % 2, 0:NT, :].bitcast(F32), ALU.subtract),
                       f"Vlo{v}", (f"Vhi{v}",))

        def po_vnew(v):
            src = qkv[:, 640:768]
            PO.add(lambda e: e.tensor_scalar(vh[:, v % 2, NT, :], src, 1.0, 1.0, ALU.mult,
                                             ALU.mult), f"vnh{v}",
                   (f"copykv{v}", if_(v >= 2, f"PV{v - 2},4")))
            PO.add(lambda e: e.tensor_tensor(vl[:, v % 2, NT, :], src,
                                             vh[:, v % 2, NT, :].bitcast(F32), ALU.subtract),
                   f"vnl{v}", (f"vnh{v}",))

        def po_rst(v, part):
            s = slice(4, 5) if part == "k" else slice(0, 4)
            last = f"sq{v},4" if part == "k" else f"sq{v},3"
            PO.add(lambda e: e.tensor_scalar(var[:, v % 2, s], ssq[:, v % 2, s], 1.0 / D, EPS,
                                             ALU.mult, ALU.add), f"var{part}{v}", (last,))
            PO.add(lambda e: e.tensor_tensor(rst[:, v % 2, s], var[:, v % 2, s], mhalf[:, s],
                                             ALU.pow), f"rst{part}{v}", (f"var{part}{v}", "mhalf"))

        warm(ACT.Sin, ("mhalf",))
        load_x(0)
        for c in range(NWR):
            load_w(0, c)
        gather_l0(0)
        gather_l0(1)
        for t in range(NT):
            gather_v(0, t)
        PE.add(warm_pe, None, ("ident",))
        l0_mm(0, None)
        angles()
        key_rows(range(1))
        load_kt(0, 0)
        split_hi(0, 0)
        split_hi(0, 1)
        sines()
        warm(ACT.Exp, ("cos",))
        split_hi(0, 2)
        split_hi(0, 3)
        split_lo(0, 0)
        split_lo(0, 1)
        load_x(1)
        load_kt(0, 1)
        load_kt(0, 2)
        load_kt(0, 3)
        for part in range(4):
            rope_table(0, part, 0)
        l0_add(0)
        l0_t(0, None)
        l0_hi(0)
        split_hi(0, 4)
        split_hi(0, 5)
        split_lo(0, 2)
        l0_lo(0)
        for c in range(3, 6):
            split_lo(0, c)
        for part in range(4):
            rope_table(1, part, 0)

        def splits(u, slot, where):
            if not 0 <= u < NU:
                return
            hk, b = divmod(u, NB)
            for op, c, at_b, at_slot, on in SPLITS:
                new = hk + 1 if b >= NB - 2 else hk
                if new == 0 and op == "hi":
                    on = "act"
                if (at_b, at_slot) != (b, slot) or (on == "pool") != (where == "pool"):
                    continue
                if new == NK or (new == 0 and c < 6):
                    continue
                (split_hi if op == "hi" else split_lo)(new, c, on)

        for u in range(-1, NU + 1):
            v, w = u + 1, u - 1
            real, nxt, old = 0 <= u < NU, v < NU, w >= 0
            lb = u + 2
            l0 = real and lb < NB
            hk, b = divmod(u, NB)
            more = hk + 1 < NK
            if real and b == NB - 3 and more:
                for c in range(NWR):
                    load_w(hk + 1, c)
            for g in range(G + 1):
                splits(u, g, "pool")
                if real and g < G and (u, g) != (0, 1):
                    pe_s(u, g)
                if (u, g) == (0, 0):
                    pe_s(0, 1)
                if nxt and g < 4:
                    pe_projq(v, g)
                if old and g + 2 < 5:
                    pe_t(w, g + 2)
                if old:
                    pe_pv(w, g)
                if real and g < G and (u, g) != (0, 1):
                    dv_max(u, g)
                if (u, g) == (0, 0):
                    dv_max(0, 1)
                if old and g + 2 < 5:
                    ac_pth(w, g + 2)
                    dv_ptl(w, g + 2)
                if nxt and g == 3:
                    ac_copyq(v)
                if real and g < G and (u, g) not in ((0, 1), (NU - 1, 3)):
                    ac_exp(u, g)
                if (u, g) == (0, 0):
                    ac_exp(0, 1)
                if v + 1 < NU and g < NT:
                    if u:
                        gather_v(v + 1, g)
                    load_kt(v + 1, g)
                if nxt and g == G:
                    dv_ropeq(v)
                if real and g >= 1 and (u, g) != (NU - 1, G):
                    dv_rcp(u, g - 1)
                    po_norm(u, g - 1)
                splits(u, g, "dve")
            if nxt:
                pe_projkv(v)
                if u == -1:
                    l0_mm(1, None)
                dv_ropeq2(v)
            if old:
                ac_oh(w)
                dv_ol(w)
                if u == NU - 1:
                    ac_exp(u, 3)
                    dv_rcp(u, 3)
                    po_norm(u, 3)
                pe_y(w, 0)
            if nxt:
                if v:
                    ac_kch(v)
                ac_copykv(v)
                dv_qadd(v)
                pe_qt(v)
                po_vsplit(v, "hi")
                if v == 0:
                    rope_table(0, 0, 1, PO)
                po_rst(v, "k")
                po_vsplit(v, "lo")
                po_vnew(v)
                if v:
                    dv_kcl(v)
                if u == 0:
                    rope_table(1, 0, 1)
                    rope_table(1, 1, 1)
                ac_sqq(v)
                dv_ropek(v)
                if v == 0:
                    ac_kch(v)
                    masks(range(1))
                    rope_table(0, 1, 1)
                    dv_kcl(v)
                    l0_add(1)
                po_rst(v, "q")
                if u == 0:
                    for t in range(NT):
                        gather_v(2, t)
                if u == -1:
                    rope_table(0, 2, 1, PO)
                    rope_table(0, 3, 1, PO)
                    gather_l0(2)
                    load_x(2)
                ac_qh(v)
                dv_ql(v)
            if l0:
                if u == 0:
                    rope_table(1, 2, 1)
                masks({0: (1,), 1: (2,), 2: (3, 4), 3: (5, 6, 7)}.get(u, ()))
                l0_mm(lb, f"max{u},2" if real else "xl0")
                l0_add(lb)
                if u == 0:
                    rope_table(1, 3, 1)
                if lb + 1 < NB:
                    gather_l0(lb + 1)
                    load_x(lb + 1)
            if u == NU - 1:
                pe_t(u, 0)
                pe_t(u, 1)
            if old:
                pe_y(w, 1)
            if l0:
                l0_t(lb, f"ol{w}" if old else "L0add1")
            if nxt:
                pe_knt(v)
                ac_knh(v)
            if u == -1:
                l0_t(1, None)
            if nxt:
                dv_knl(v)
            if u == -1:
                l0_hi(1)
                l0_lo(1)
            if l0:
                l0_hi(lb)
                l0_lo(lb)
            if real and b == 2 and more:
                key_rows(range(hk + 1, hk + 2))
            splits(u, G + 1, "pool")
            splits(u, G + 1, "dve")
            if real:
                if u < NU - 1:
                    pe_t(u, 0)
                    pe_t(u, 1)
                ac_pth(u, 0)
                dv_ptl(u, 0)
                ac_pth(u, 1)
            if u == NU - 1:
                dv_ptl(u, 1)
            if old:
                dv_yadd(w)
                if w >= NU - NB:
                    bb = w % NB
                    SP.dma(lambda e, bb=bb: e.dma_start(out[bb], acc[:, bb, :]), d_out, f"out{bb}",
                           (f"yadd{w}",))
            if real and u < NU - 1:
                dv_ptl(u, 1)

        block = ctx.enter_context(nc.Block())

        @block.sync
        def _(e):
            SP.emit(e)
            e.wait_ge(d_out, 16 * NB)

        @block.gpsimd
        def _(e):
            PO.emit(e)

        @block.scalar
        def _(e):
            AC.emit(e)

        @block.vector
        def _(e):
            DV.emit(e)

        @block.tensor
        def _(e):
            PE.emit(e)


def kernel(x, itok_B_0_15, itok_Bx16_0_63, itok_B_207_1644, L0_cond_weight, L1_cond_Wq, L1_cond_Wk,
           L1_cond_Wv, L1_cond_Wo, L1_cond_q_norm_w, L1_cond_k_norm_w, L1_cond_k_cache,
           L1_cond_v_cache):
    import concourse.bacc as bacc
    from concourse.bass_utils import run_bass_kernel_spmd

    c = np.ascontiguousarray
    x = np.asarray(x)
    wq, wk, wv, wo = (np.asarray(w) for w in (L1_cond_Wq, L1_cond_Wk, L1_cond_Wv, L1_cond_Wo))

    def by_head(w, n):
        return w.reshape(NK, n, 4, P).transpose(0, 3, 2, 1)

    wq_h = by_head(wq, 512).reshape(NK, P, 2048)
    wkv_h = np.concatenate([by_head(wk, 128), by_head(wv, 128)], axis=3).reshape(NK, P, 1024)
    wo_h = wo.reshape(HID, NK, G, D).transpose(1, 3, 2, 0).reshape(NK, P, 2048)
    inv = (np.float32(1.0) / np.float32(10000.0) ** (np.arange(0, D, 2, dtype=np.float32) /
                                                    np.float32(D))).astype(np.float32)
    p = np.arange(P)
    consts = np.concatenate([np.stack([p, p % 32, p], axis=1), np.broadcast_to(inv, (P, 64))],
                            axis=1).astype(np.float32)
    iota = np.broadcast_to(np.arange(512, dtype=np.float32), (P, 512))
    arrays = {
        "x": c(x),
        "xt": c(x.reshape(NB, P, 4, P).transpose(0, 3, 2, 1)),
        "lw": c(np.asarray(L0_cond_weight).transpose(0, 2, 1).reshape(16 * HID, HID)),
        "wall": c(np.concatenate([wq_h, wkv_h, wo_h], axis=2)),
        "kt": c(np.asarray(L1_cond_k_cache).transpose(2, 0, 3, 1)),
        "vrows": c(np.asarray(L1_cond_v_cache).transpose(2, 0, 1, 3).reshape(NK * 2048, D)),
        "ids_lens": c(np.concatenate([np.asarray(itok_B_0_15), np.asarray(itok_B_207_1644)])),
        "table": c(np.asarray(itok_Bx16_0_63).reshape(NB * NT, 4).transpose(1, 0)),
        "pages": c(np.asarray(itok_Bx16_0_63).reshape(1, NB * NPG)),
        "qkw": c(np.concatenate([np.asarray(L1_cond_q_norm_w), np.asarray(L1_cond_k_norm_w)])),
        "consts": c(consts),
        "iota": c(iota),
    }
    nc = bacc.Bacc("TRN2", target_bir_lowering=False, num_devices=1)
    ins = {}
    args = []
    for name, a in arrays.items():
        ins[f"in_{name}"] = a
        args.append(nc.dram_tensor(f"in_{name}", a.shape, mybir.dt.from_np(a.dtype),
                                   kind="ExternalInput").ap())
    o = nc.dram_tensor("out_0", (NB, P, HID), F32, kind="ExternalOutput").ap()
    build(nc, *args, o)
    r = run_bass_kernel_spmd(nc, [ins], core_ids=[0])
    return r.results[0]["out_0"]
```
